# Optimizing a Trainium2 kernel written in Bass

```python
import numpy as np
import jax
import jax.numpy as jnp

def _softmax(x, axis=-1):
    return jax.nn.softmax(x, axis=axis)

def _gelu(x):
    return jax.nn.gelu(x, approximate=True)

def _silu(x):
    return jax.nn.silu(x)

def _sigmoid(x):
    return jax.nn.sigmoid(x)

def _layernorm(x, axis=-1, eps=1e-05):
    m = jnp.mean(x, axis=axis, keepdims=True)
    v = jnp.var(x, axis=axis, keepdims=True)
    return (x - m) / jnp.sqrt(v + eps)

def _scatter_add(tgt, idx, src, axis=0):
    return tgt.at[idx].add(src)

def _segment_sum(src, seg, n):
    return jax.ops.segment_sum(src, seg, n)
kernel_name = 'mk_dlrm_tower_d1_rec_r8_064fab'

def setup_inputs(seed: int=0):
    np.random.seed(seed)
    _w = jnp.asarray

    def _rec_inputs():
        import jax
        import jax.numpy as jnp
        _tk = jax.random.key(seed)
        ids = jnp.stack([jax.random.randint(jax.random.fold_in(_tk, 200 + f), (512,), 0, v, jnp.int32) for f, v in enumerate([12500, 12500, 1250, 1000, 125000, 1000, 125000, 1000, 12500, 1250, 12500, 12500, 12500, 1250, 12500, 125000, 12500, 1000, 1250, 1250, 1250, 1000, 1000, 1000, 1000, 1000])], axis=1)
        tbl_0 = 0.05 * jax.random.normal(jax.random.fold_in(_tk, 500 + 0), (12500, 64), jnp.float32)
        tbl_1 = 0.05 * jax.random.normal(jax.random.fold_in(_tk, 500 + 1), (12500, 64), jnp.float32)
        tbl_2 = 0.05 * jax.random.normal(jax.random.fold_in(_tk, 500 + 2), (1250, 64), jnp.float32)
        tbl_3 = 0.05 * jax.random.normal(jax.random.fold_in(_tk, 500 + 3), (1000, 64), jnp.float32)
        tbl_4 = 0.05 * jax.random.normal(jax.random.fold_in(_tk, 500 + 4), (125000, 64), jnp.float32)
        tbl_5 = 0.05 * jax.random.normal(jax.random.fold_in(_tk, 500 + 5), (1000, 64), jnp.float32)
        tbl_6 = 0.05 * jax.random.normal(jax.random.fold_in(_tk, 500 + 6), (125000, 64), jnp.float32)
        tbl_7 = 0.05 * jax.random.normal(jax.random.fold_in(_tk, 500 + 7), (1000, 64), jnp.float32)
        tbl_8 = 0.05 * jax.random.normal(jax.random.fold_in(_tk, 500 + 8), (12500, 64), jnp.float32)
        tbl_9 = 0.05 * jax.random.normal(jax.random.fold_in(_tk, 500 + 9), (1250, 64), jnp.float32)
        tbl_10 = 0.05 * jax.random.normal(jax.random.fold_in(_tk, 500 + 10), (12500, 64), jnp.float32)
        tbl_11 = 0.05 * jax.random.normal(jax.random.fold_in(_tk, 500 + 11), (12500, 64), jnp.float32)
        tbl_12 = 0.05 * jax.random.normal(jax.random.fold_in(_tk, 500 + 12), (12500, 64), jnp.float32)
        tbl_13 = 0.05 * jax.random.normal(jax.random.fold_in(_tk, 500 + 13), (1250, 64), jnp.float32)
        tbl_14 = 0.05 * jax.random.normal(jax.random.fold_in(_tk, 500 + 14), (12500, 64), jnp.float32)
        tbl_15 = 0.05 * jax.random.normal(jax.random.fold_in(_tk, 500 + 15), (125000, 64), jnp.float32)
        tbl_16 = 0.05 * jax.random.normal(jax.random.fold_in(_tk, 500 + 16), (12500, 64), jnp.float32)
        tbl_17 = 0.05 * jax.random.normal(jax.random.fold_in(_tk, 500 + 17), (1000, 64), jnp.float32)
        tbl_18 = 0.05 * jax.random.normal(jax.random.fold_in(_tk, 500 + 18), (1250, 64), jnp.float32)
        tbl_19 = 0.05 * jax.random.normal(jax.random.fold_in(_tk, 500 + 19), (1250, 64), jnp.float32)
        tbl_20 = 0.05 * jax.random.normal(jax.random.fold_in(_tk, 500 + 20), (1250, 64), jnp.float32)
        tbl_21 = 0.05 * jax.random.normal(jax.random.fold_in(_tk, 500 + 21), (1000, 64), jnp.float32)
        tbl_22 = 0.05 * jax.random.normal(jax.random.fold_in(_tk, 500 + 22), (1000, 64), jnp.float32)
        tbl_23 = 0.05 * jax.random.normal(jax.random.fold_in(_tk, 500 + 23), (1000, 64), jnp.float32)
        tbl_24 = 0.05 * jax.random.normal(jax.random.fold_in(_tk, 500 + 24), (1000, 64), jnp.float32)
        tbl_25 = 0.05 * jax.random.normal(jax.random.fold_in(_tk, 500 + 25), (1000, 64), jnp.float32)
        _rk = jax.random.fold_in(_tk, 7)
        r_dense_t = 7.22013e-05 + 1.00017 * jax.random.normal(jax.random.fold_in(_rk, 101), (512, 256), jnp.float32)
        W_top1 = 0.0360844 * jax.random.normal(jax.random.fold_in(_tk, 801), (768, 512), jnp.float32)
        W_top2 = 0.0441942 * jax.random.normal(jax.random.fold_in(_tk, 802), (512, 256), jnp.float32)
        W_top3 = 0.0625 * jax.random.normal(jax.random.fold_in(_tk, 803), (256, 1), jnp.float32)
        b_top1 = jnp.zeros((512,), jnp.float32)
        b_top2 = jnp.zeros((256,), jnp.float32)
        return (r_dense_t, ids, tbl_0, tbl_1, tbl_2, tbl_3, tbl_4, tbl_5, tbl_6, tbl_7, tbl_8, tbl_9, tbl_10, tbl_11, tbl_12, tbl_13, tbl_14, tbl_15, tbl_16, tbl_17, tbl_18, tbl_19, tbl_20, tbl_21, tbl_22, tbl_23, tbl_24, tbl_25, W_top1, b_top1, W_top2, b_top2, W_top3)
    r_dense_t, ids, tbl_0, tbl_1, tbl_2, tbl_3, tbl_4, tbl_5, tbl_6, tbl_7, tbl_8, tbl_9, tbl_10, tbl_11, tbl_12, tbl_13, tbl_14, tbl_15, tbl_16, tbl_17, tbl_18, tbl_19, tbl_20, tbl_21, tbl_22, tbl_23, tbl_24, tbl_25, W_top1, b_top1, W_top2, b_top2, W_top3 = _rec_inputs()

    def _L0_rec_setup():
        import jax, jax.numpy as jnp
        import numpy as np
        EPS = 1e-05
        NI = 33
        TRIL_I, TRIL_J = np.tril_indices(NI, k=-1)

        def layer_norm(x, g, b):
            m = jnp.mean(x, axis=-1, keepdims=True)
            v = jnp.mean(jnp.square(x - m), axis=-1, keepdims=True)
            return (x - m) * jax.lax.rsqrt(v + EPS) * g + b
        key = jax.random.key(seed)
        ks = jax.random.split(key, 8)
        B, D_DENSE, N_SP, D_SP = (4096, 256, 26, 64)
        E, PROJ, MAXD, NFLAT = (128, 32, 512, 528)
        dense_t = jax.random.normal(ks[0], (B, D_DENSE), dtype=jnp.float32)
        sparse_t = jax.random.normal(ks[1], (B, N_SP, D_SP), dtype=jnp.float32)
        Wd = jax.random.normal(ks[2], (E, D_DENSE), dtype=jnp.float32) / np.sqrt(D_DENSE)
        Ws = jax.random.normal(ks[3], (E, D_SP), dtype=jnp.float32) / np.sqrt(D_SP)
        Wsi = jax.random.normal(ks[4], (PROJ, N_SP), dtype=jnp.float32) / np.sqrt(N_SP)
        Wl = jax.random.normal(ks[5], (MAXD, NFLAT), dtype=jnp.float32) / np.sqrt(NFLAT)
        gd = jnp.ones((E,), jnp.float32)
        bd = jnp.zeros((E,), jnp.float32)
        gs = jnp.ones((E,), jnp.float32)
        bs = jnp.zeros((E,), jnp.float32)
        gsi = jnp.ones((PROJ,), jnp.float32)
        bsi = jnp.zeros((PROJ,), jnp.float32)
        gl = jnp.ones((MAXD,), jnp.float32)
        bl = jnp.zeros((MAXD,), jnp.float32)
        return {'dense_t': dense_t, 'sparse_t': sparse_t, 'Wd': Wd, 'gd': gd, 'bd': bd, 'Ws': Ws, 'gs': gs, 'bs': bs, 'Wsi': Wsi, 'gsi': gsi, 'bsi': bsi, 'Wl': Wl, 'gl': gl, 'bl': bl, 'dims_in_use': 384}
    _L0_rec_all = _L0_rec_setup()
    _L0_rec_in = {k: v for k, v in _L0_rec_all.items() if k in ('Wd', 'gd', 'bd', 'Ws', 'gs', 'bs', 'Wsi', 'gsi', 'bsi', 'Wl', 'gl', 'bl')}
    del _L0_rec_all
    return {'r_dense_t': r_dense_t, 'ids': ids, 'tbl_0': tbl_0, 'tbl_1': tbl_1, 'tbl_2': tbl_2, 'tbl_3': tbl_3, 'tbl_4': tbl_4, 'tbl_5': tbl_5, 'tbl_6': tbl_6, 'tbl_7': tbl_7, 'tbl_8': tbl_8, 'tbl_9': tbl_9, 'tbl_10': tbl_10, 'tbl_11': tbl_11, 'tbl_12': tbl_12, 'tbl_13': tbl_13, 'tbl_14': tbl_14, 'tbl_15': tbl_15, 'tbl_16': tbl_16, 'tbl_17': tbl_17, 'tbl_18': tbl_18, 'tbl_19': tbl_19, 'tbl_20': tbl_20, 'tbl_21': tbl_21, 'tbl_22': tbl_22, 'tbl_23': tbl_23, 'tbl_24': tbl_24, 'tbl_25': tbl_25, 'W_top1': W_top1, 'b_top1': b_top1, 'W_top2': W_top2, 'b_top2': b_top2, 'W_top3': W_top3, 'L0_rec_Wd': _L0_rec_in['Wd'], 'L0_rec_gd': _L0_rec_in['gd'], 'L0_rec_bd': _L0_rec_in['bd'], 'L0_rec_Ws': _L0_rec_in['Ws'], 'L0_rec_gs': _L0_rec_in['gs'], 'L0_rec_bs': _L0_rec_in['bs'], 'L0_rec_Wsi': _L0_rec_in['Wsi'], 'L0_rec_gsi': _L0_rec_in['gsi'], 'L0_rec_bsi': _L0_rec_in['bsi'], 'L0_rec_Wl': _L0_rec_in['Wl'], 'L0_rec_gl': _L0_rec_in['gl'], 'L0_rec_bl': _L0_rec_in['bl']}

def reference(r_dense_t, ids, tbl_0, tbl_1, tbl_2, tbl_3, tbl_4, tbl_5, tbl_6, tbl_7, tbl_8, tbl_9, tbl_10, tbl_11, tbl_12, tbl_13, tbl_14, tbl_15, tbl_16, tbl_17, tbl_18, tbl_19, tbl_20, tbl_21, tbl_22, tbl_23, tbl_24, tbl_25, W_top1, b_top1, W_top2, b_top2, W_top3, L0_rec_Wd, L0_rec_gd, L0_rec_bd, L0_rec_Ws, L0_rec_gs, L0_rec_bs, L0_rec_Wsi, L0_rec_gsi, L0_rec_bsi, L0_rec_Wl, L0_rec_gl, L0_rec_bl):
    import jax
    import jax.numpy as jnp

    def _L0_rec_ref(dense_t, sparse_t, Wd, gd, bd, Ws, gs, bs, Wsi, gsi, bsi, Wl, gl, bl, dims_in_use):
        import jax, jax.numpy as jnp
        import numpy as np
        EPS = 1e-05
        NI = 33
        TRIL_I, TRIL_J = np.tril_indices(NI, k=-1)

        def layer_norm(x, g, b):
            m = jnp.mean(x, axis=-1, keepdims=True)
            v = jnp.mean(jnp.square(x - m), axis=-1, keepdims=True)
            return (x - m) * jax.lax.rsqrt(v + EPS) * g + b
        x = layer_norm(dense_t @ Wd.T, gd, bd)
        y = layer_norm(jnp.einsum('bnd,ed->bne', sparse_t, Ws), gs, bs)
        y = jnp.einsum('bne,pn->bep', y, Wsi)
        y = layer_norm(y, gsi, bsi)
        y = jnp.swapaxes(y, 1, 2)
        T = jnp.concatenate([x[:, None, :], y], axis=1)
        Z = jnp.einsum('bnd,bmd->bnm', T, T)
        Zflat = Z[:, TRIL_I, TRIL_J]
        out = layer_norm(Zflat @ Wl.T, gl, bl)
        maxd = out.shape[-1]
        mask = (jnp.arange(maxd) < dims_in_use).astype(out.dtype)
        return out * mask
    e = jnp.stack([tbl_0[ids[:, 0]], tbl_1[ids[:, 1]], tbl_2[ids[:, 2]], tbl_3[ids[:, 3]], tbl_4[ids[:, 4]], tbl_5[ids[:, 5]], tbl_6[ids[:, 6]], tbl_7[ids[:, 7]], tbl_8[ids[:, 8]], tbl_9[ids[:, 9]], tbl_10[ids[:, 10]], tbl_11[ids[:, 11]], tbl_12[ids[:, 12]], tbl_13[ids[:, 13]], tbl_14[ids[:, 14]], tbl_15[ids[:, 15]], tbl_16[ids[:, 16]], tbl_17[ids[:, 17]], tbl_18[ids[:, 18]], tbl_19[ids[:, 19]], tbl_20[ids[:, 20]], tbl_21[ids[:, 21]], tbl_22[ids[:, 22]], tbl_23[ids[:, 23]], tbl_24[ids[:, 24]], tbl_25[ids[:, 25]]], axis=1)
    z = _L0_rec_ref(r_dense_t, e, L0_rec_Wd, L0_rec_gd, L0_rec_bd, L0_rec_Ws, L0_rec_gs, L0_rec_bs, L0_rec_Wsi, L0_rec_gsi, L0_rec_bsi, L0_rec_Wl, L0_rec_gl, L0_rec_bl, 384)
    z = z.reshape(z.shape[0], -1)
    h = jnp.concatenate([z, r_dense_t], axis=1)
    h = jnp.maximum(h @ W_top1 + b_top1, 0.0)
    h = jnp.maximum(h @ W_top2 + b_top2, 0.0)
    y = h @ W_top3
    return y

_drawn_inputs = setup_inputs


def setup_inputs(seed=0):
    import zlib

    import numpy as np

    out = dict(_drawn_inputs(seed))
    spreads = {'b_top1': (0.0, 0.1),
     'b_top2': (0.0, 0.1),
     'L0_rec_gd': (1.0, 0.6),
     'L0_rec_bd': (0.0, 0.8),
     'L0_rec_gs': (1.0, 0.6),
     'L0_rec_bs': (0.0, 0.1),
     'L0_rec_gsi': (1.0, 0.2),
     'L0_rec_bsi': (0.0, 0.1),
     'L0_rec_gl': (1.0, 0.2),
     'L0_rec_bl': (0.0, 0.1)}
    factors = {}
    for name, (base, spread) in spreads.items():
        noise = np.random.default_rng([zlib.crc32(name.encode()), seed]).standard_normal(out[name].shape)
        drawn = base * np.exp(spread * noise) if base else spread * noise
        out[name] = jnp.asarray(drawn.astype(out[name].dtype))
    for name, factor in factors.items():
        out[name] = (out[name] * factor).astype(out[name].dtype)
    return out
```

```python
from contextlib import ExitStack

import numpy as np

import concourse.bass as bass
from concourse import mybir

F32 = mybir.dt.float32
I32 = mybir.dt.int32
ALU = mybir.AluOpType
ACT = mybir.ActivationFunctionType
AX = mybir.AxisListType

P = 128
VOCAB = [12500, 12500, 1250, 1000, 125000, 1000, 125000, 1000, 12500, 1250, 12500, 12500, 12500,
         1250, 12500, 125000, 12500, 1000, 1250, 1250, 1250, 1000, 1000, 1000, 1000, 1000]
B = 512
NF = len(VOCAB)
D = 64
E = 128
PR = 32
DD = 256
KEPT = 384
MAXD = 512
H1, H2 = 512, 256
EPS = 1e-5

BLK = 64
NBLK = B // BLK
QB = 16
QPB = BLK // QB
QPT = 2 * QPB
NT = B // P
NQ = NT * QPT
CPB = BLK * NF // P
CPT = 2 * CPB
assert CPB * P == BLK * NF

LAST = [-(-(QB * (q + 1) * NF) // P) - 1 for q in range(QPB)]
CHUNKS = [list(range(LAST[q - 1] + 1 if q else 0, LAST[q] + 1)) for q in range(QPB)]
SPAN = [(P * c // NF, -(-(P * (c + 1)) // NF)) for c in range(CPB)]
BDCOL = np.cumsum([0] + [b - a for a, b in SPAN]).tolist()
NCOL = BDCOL[-1]

TRI = [
    (0, [[16 * PR + 16, 2], [PR, 8], [1, 8]]),
    (8 * PR, [[PR, 8], [1, 16]]),
    (16 * PR, [[PR, 8], [1, 16]]),
    (24 * PR, [[PR, 4], [1, PR]]),
    (28 * PR, [[PR, 4], [1, PR]]),
]
NK = len(TRI)

COLS = {}
NPAR = 0
for _name, _n in [("gs", 1), ("gd", 1), ("bd", 1), ("gl", KEPT // P), ("bl", KEPT // P),
                  ("b1", H1 // P), ("b2", H2 // P), ("w3", H2 // P), ("gsi", PR), ("bsi", PR),
                  ("bs", P), ("ident", P), ("mask", NCOL), ("wsi", CPB * PR), ("ws", 2 * P)]:
    COLS[_name] = (NPAR, _n)
    NPAR += _n


def tri_pairs():
    out = []
    for off, ap in TRI:
        places = [off]
        for step, n in ap:
            places = [x + step * i for x in places for i in range(n)]
        out += [(x // PR, x % PR) for x in places]
    return out


def real(n):
    return not isinstance(n, int) or n >= 0


def dlrm(nc, ids, offs, table, params, dense, wlin, w1, w2, out):
    with ExitStack() as ctx:
        def sb(name, shape, dt=F32):
            return ctx.enter_context(nc.sbuf_tensor(name, shape, dt))

        def sem(name):
            return ctx.enter_context(nc.semaphore(name))

        ids_sb = sb("ids_sb", [P, NT * CPT], I32)
        offs_sb = sb("offs_sb", [P, NT * CPT], I32)
        idx = sb("idx", [P, NT * CPT], I32)
        par = sb("par", [P, NPAR])
        dense_sb = sb("dense_sb", [P, 2, P + B])
        wl = sb("wl", [P, NK, MAXD])
        w1s = sb("w1s", [P, (KEPT + DD) // P, H1])
        w2s = sb("w2s", [P, H1 // P, H2])
        eps = sb("eps", [P, 1])
        bd = sb("bd", [P, NCOL * PR])
        rows = sb("rows", [P, CPT, D])
        rowsT = sb("rowsT", [P, 2, 2, P])
        sqa = sb("sqa", [P, 2, 4, P])
        va = sb("va", [P, 2, 4])
        sda = sb("sda", [P, 2, 4])
        ra = sb("ra", [P, 2, 4])
        ya = sb("ya", [P, 4, 4, P])
        bw = sb("bw", [P, PR])
        yb = sb("yb", [P, 2, QB, PR])
        sqb = sb("sqb", [P, 2, QB, PR])
        vb = sb("vb", [P, 2, QB])
        sdb = sb("sdb", [P, 2, QB])
        rb = sb("rb", [P, 2, QB])
        tt = sb("tt", [P, 2, BLK, PR + 1])
        xT = sb("xT", [P, B])
        zs = sb("zs", [P, 2, QB, PR])
        zr = sb("zr", [P, PR * PR])
        zp = sb("zp", [P, 3, P])
        zT = sb("zT", [P, NK, P])
        sqc = sb("sqc", [P, MAXD])
        vc = sb("vc", [P, 1])
        sdc = sb("sdc", [P, 1])
        rc = sb("rc", [P, 1])
        on = sb("on", [P, KEPT])
        oT = sb("oT", [P, KEPT // P, P])
        h1 = sb("h1", [P, H1 // P, P])
        h2 = sb("h2", [P, H2 // P, P])
        ys = sb("ys", [1, B])
        cen = sb("cen", [P, 32])
        xsq = sb("xsq", [P, NT, P])
        xv = sb("xv", [P, 3, NT])
        xn = sb("xn", [P, NT, P])
        wk = sb("wk", [P, PR])

        p_tr = ctx.enter_context(nc.psum_tensor("p_tr", [P, 4, P], F32))
        p_ya = [ctx.enter_context(nc.psum_tensor(f"p_ya{i}", [P, 4, P], F32)) for i in range(2)]
        p_yb = [ctx.enter_context(nc.psum_tensor(f"p_yb{i}", [P, QB, PR], F32)) for i in range(2)]
        p_z = ctx.enter_context(nc.psum_tensor("p_z", [P, QB, PR], F32))
        p_m = [ctx.enter_context(nc.psum_tensor(f"p_m{i}", [P, 4, P], F32)) for i in range(2)]
        zdram = nc.dram_tensor("zdram", [NT, P, PR * PR], F32, kind="Internal").ap()

        ids_in = sem("ids_in")
        par_in = sem("par_in")
        dense_in = sem("dense_in")
        wl_in = sem("wl_in")
        w1_in = sem("w1_in")
        w2_in = sem("w2_in")
        idx_done = sem("idx_done")
        gathered = [sem(f"gathered{k}") for k in range(QPT)]
        zeroed = sem("zeroed")
        prep = sem("prep")
        ws_done = sem("ws_done")
        bd_done = sem("bd_done")
        bw_mm = sem("bw_mm")
        bw_done = sem("bw_done")
        wl_done = sem("wl_done")
        x_mm = sem("x_mm")
        x_sq = sem("x_sq")
        x_var = sem("x_var")
        x_sd = sem("x_sd")
        x_n = sem("x_n")
        x_tr = sem("x_tr")
        x_done = sem("x_done")
        tr_done = sem("tr_done")
        trE_done = sem("trE_done")
        ya_mm = sem("ya_mm")
        sqa_done = sem("sqa_done")
        va_done = sem("va_done")
        sda_done = sem("sda_done")
        ra_done = sem("ra_done")
        ya_done = sem("ya_done")
        yb_mm = sem("yb_mm")
        yb_done = sem("yb_done")
        sqb_done = sem("sqb_done")
        vb_done = sem("vb_done")
        sdb_done = sem("sdb_done")
        rb_done = sem("rb_done")
        t_done = sem("t_done")
        x_put = sem("x_put")
        aff_done = sem("aff_done")
        gram_mm = sem("gram_mm")
        zs_done = sem("zs_done")
        z_stored = [sem(f"z_stored{i}") for i in range(2)]
        z_in = sem("z_in")
        zp_done = sem("zp_done")
        ztr_mm = sem("ztr_mm")
        zT_done = sem("zT_done")
        lin_mm = sem("lin_mm")
        sqc_done = sem("sqc_done")
        sdc_done = sem("sdc_done")
        rc_done = sem("rc_done")
        on_done = sem("on_done")
        otr_mm = sem("otr_mm")
        oT_done = sem("oT_done")
        h1_mm = sem("h1_mm")
        h1_done = sem("h1_done")
        h2_mm = sem("h2_mm")
        h2_done = sem("h2_done")
        y_mm = sem("y_mm")
        y_done = sem("y_done")
        y_out = sem("y_out")

        def col(name, i=0, n=1):
            a = COLS[name][0] + i
            return par[:, a:a + n]

        ident = col("ident", 0, P)
        ws = [col("ws", P * g, P) for g in range(2)]

        def tri(k):
            off, ap = TRI[k]
            v = zr[:, :]
            return bass.AP(tensor=v.tensor, offset=v.offset + off, ap=[v.ap[0], *ap])

        def packed(k):
            return zp[:, k, :] if k < 3 else zr[:, PR * (24 + 4 * (k - 3)):PR * (28 + 4 * (k - 3))]

        def blocks_at(t, k, lag):
            if (k - lag) % QPB:
                return None
            b = (k - lag) // QPB
            n = 2 * t + b
            return (n, b % 2) if real(n) and (not isinstance(n, int) or n < NBLK) else None

        def has(n):
            return real(n) and (not isinstance(n, int) or n < NQ)

        def through(eng, iteration):
            iteration(0)
            iteration(1)
            with eng.Fori(2, NT) as t:
                iteration(t)
            iteration(NT)
            iteration(NT + 1)

        def back_at(t):
            return t - 2 if real(t - 2) else None

        block = ctx.enter_context(nc.Block())

        @block.sync
        def _(sp):
            sp.dma_start(ids_sb[:, :], ids).then_inc(ids_in, 16)
            sp.dma_start(offs_sb[:, :], offs).then_inc(ids_in, 16)
            sp.dma_start(par[:, :], params).then_inc(par_in, 16)
            sp.dma_start(dense_sb[:, :, :], dense).then_inc(dense_in, 16)
            sp.dma_start(wl[:, :, :], wlin).then_inc(wl_in, 16)
            sp.dma_start(w1s[:, :, :], w1).then_inc(w1_in, 16)
            sp.dma_start(w2s[:, :, :], w2).then_inc(w2_in, 16)

            def store(n, par_, t, half):
                sp.wait_ge(zs_done, n + 1)
                dst = zdram[t, half * BLK:(half + 1) * BLK, :].rearrange(
                    "(b q) (i j) -> (q i) b j", q=4, j=PR)
                sp.dma_start(dst, zs[:, par_, :, :]).then_inc(z_stored[par_], 16)

            def iteration(t):
                if isinstance(t, int) and not 1 <= t <= NT:
                    return
                for half in range(2):
                    store(2 * t - 2 + half, half, t - 1, half)
                for half in range(2):
                    sp.wait_ge(z_stored[half], 16 * t)
                if not isinstance(t, int) or t >= 2:
                    sp.wait_ge(ztr_mm, t - 1)
                sp.dma_start(zr[:, :], zdram[t - 1]).then_inc(z_in, 16)

            through(sp, iteration)
            sp.wait_ge(y_done, NT)
            sp.dma_start(out.rearrange("b o -> o b"), ys[:, :]).then_inc(y_out, 16)
            sp.wait_ge(y_out, 16)

        @block.gpsimd
        def _(pool):
            pool.wait_ge(idx_done, 1)
            for t in range(NT):
                for k in range(QPT):
                    if t:
                        pool.wait_ge(tr_done, QPT * (t - 1) + k + 1)
                    for c in CHUNKS[k % QPB]:
                        j = CPB * (k // QPB) + c
                        pool.indirect_dma_start(
                            rows[:, j, :], None, table,
                            bass.IndirectOffsetOnAxis(ap=idx[:, CPT * t + j:CPT * t + j + 1], axis=0),
                        ).then_inc(gathered[k], 16)

        @block.tensor
        def _(pe):
            def transposes(t, k):
                n = QPT * t + k
                pe.wait_ge(gathered[k], (t + 1) * (16 * len(CHUNKS[k % QPB])))
                if real(n - 1):
                    pe.wait_ge(trE_done, n)
                ch = [CPB * (k // QPB) + c for c in CHUNKS[k % QPB]]
                for u in range(2):
                    two = len(ch) > 2 * u + 1
                    src = rows[:, ch[2 * u]:ch[2 * u] + (2 if two else 1), :].rearrange("p c d -> p (c d)")
                    last = pe.transpose(p_tr[0:D * (2 if two else 1), u, :], src, ident)
                last.then_inc(tr_done, 1)

            def project_rows(t, k, n):
                pe.wait_ge(trE_done, n + 1)
                if real(n - 2):
                    pe.wait_ge(ya_done, n - 1)
                for i, c in enumerate(CHUNKS[k % QPB]):
                    last = pe.matmul(p_ya[k % 2][:, i, :], rowsT[:, k % 2, i // 2, :], ws[i % 2],
                                     start=True, stop=True)
                last.then_inc(ya_mm, 1)

            def project_fields(t, k, n):
                pe.wait_ge(ya_done, n + 1)
                if real(n - 2):
                    pe.wait_ge(yb_done, n - 1)
                q = k % QPB
                lo, hi = QB * q, QB * (q + 1)
                parts = [c for c in range(CPB) if SPAN[c][0] < hi and SPAN[c][1] > lo and c <= LAST[q]]
                for c in parts:
                    a, b = max(SPAN[c][0], lo), min(SPAN[c][1], hi)
                    own = c in CHUNKS[q]
                    kk = k if own else k - 1
                    i = CHUNKS[q].index(c) if own else CHUNKS[q - 1].index(c)
                    r = (BDCOL[c] + a - SPAN[c][0]) * PR
                    last = pe.matmul(p_yb[k % 2][:, a - lo:b - lo, :], ya[:, kk % 4, i, :],
                                     bd[:, r:r + (b - a) * PR], start=(c == parts[0]),
                                     stop=(c == parts[-1]), skip_group_check=True)
                last.then_inc(yb_mm, 1)

            def gram(n, par_, half):
                if half == 0:
                    pe.wait_ge(aff_done, n + 1)
                    if real(n - 1):
                        pe.wait_ge(zs_done, n)
                for b in range(BLK // 2 * half, BLK // 2 * (half + 1)):
                    q = b % 4
                    last = pe.matmul(p_z[PR * q:PR * (q + 1), b // 4, :], tt[:, par_, b, 1:PR + 1],
                                     tt[:, par_, b, 0:PR], start=True, stop=True)
                if half == 1:
                    last.then_inc(gram_mm, 1)

            def back(u, k):
                if k == 1:
                    pe.wait_ge(zp_done, u + 1)
                    if real(u - 1):
                        pe.wait_ge(y_done, u)
                    for j in range(NK):
                        last = pe.transpose(p_m[j // 4][:, j % 4, :], packed(j), ident)
                    last.then_inc(ztr_mm, 1)
                if k == 2:
                    pe.wait_ge(zT_done, u + 1)
                    if isinstance(u, int) and u == 0:
                        pe.wait_ge(wl_done, 1)
                    for j in range(NK):
                        last = pe.matmul(p_m[0][:, :, :], zT[:, j, :], wl[:, j, :],
                                         start=(j == 0), stop=(j == NK - 1))
                    last.then_inc(lin_mm, 1)
                if k == 4:
                    pe.wait_ge(on_done, u + 1)
                    for j in range(KEPT // P):
                        last = pe.transpose(p_m[1][:, j, :], on[:, P * j:P * (j + 1)], ident)
                    last.then_inc(otr_mm, 1)
                if k == 5:
                    pe.wait_ge(oT_done, u + 1)
                    if isinstance(u, int) and u == 0:
                        pe.wait_ge(w1_in, 16)
                    for m in range(H1 // P):
                        for j in range(5):
                            rhs = oT[:, j, :] if j < 3 else dense_sb[:, j - 3, bass.ds(P + P * u, P)]
                            last = pe.matmul(p_m[0][:, m, :], w1s[:, j, P * m:P * (m + 1)], rhs,
                                             start=(j == 0), stop=(j == 4))
                    last.then_inc(h1_mm, 1)
                if k == 6:
                    pe.wait_ge(h1_done, u + 1)
                    if isinstance(u, int) and u == 0:
                        pe.wait_ge(w2_in, 16)
                    for m in range(H2 // P):
                        for j in range(H1 // P):
                            last = pe.matmul(p_m[1][:, m, :], w2s[:, j, P * m:P * (m + 1)], h1[:, j, :],
                                             start=(j == 0), stop=(j == H1 // P - 1))
                    last.then_inc(h2_mm, 1)
                if k == 7:
                    pe.wait_ge(h2_done, u + 1)
                    for j in range(H2 // P):
                        last = pe.matmul(p_m[0][0:1, 0, :], col("w3", j), h2[:, j, :],
                                         start=(j == 0), stop=(j == H2 // P - 1))
                    last.then_inc(y_mm, 1)

            def iteration(t):
                for k in range(QPT):
                    n = QPT * t + k
                    if has(n):
                        transposes(t, k)
                    if has(n - 1):
                        project_rows(t, k - 1, n - 1)
                    if has(n - 2):
                        project_fields(t, k - 2, n - 2)
                    for half in range(2):
                        if (found := blocks_at(t, k, 9 + half)):
                            gram(*found, half)
                    if back_at(t) is not None:
                        back(back_at(t), k)

            pe.wait_ge(prep, 1)
            for t in range(NT):
                for j in range(2):
                    last = pe.matmul(p_m[0][:, t, :], dense_sb[:, j, P + P * t:P + P * (t + 1)],
                                     dense_sb[:, j, 0:P], start=(j == 0), stop=(j == 1))
            last.then_inc(x_mm, 1)
            pe.wait_ge(prep, 2)
            pe.matmul(p_m[1][:, 0, 0:PR], col("bs", 0, P), wk[:, :], start=True, stop=True).then_inc(bw_mm, 1)
            pe.wait_ge(bw_done, 1)
            pe.wait_ge(x_n, 1)
            for t in range(NT):
                last = pe.transpose(p_m[1][:, t, :], xn[:, t, :], ident)
            last.then_inc(x_tr, 1)
            pe.wait_ge(x_done, 1)
            pe.wait_ge(zeroed, 2)
            pe.wait_ge(ws_done, 1)
            pe.wait_ge(bd_done, 1)
            through(pe, iteration)

        @block.scalar
        def _(act):
            def evacuate_rows(t, k, n):
                act.wait_ge(tr_done, n + 1)
                if real(n - 2):
                    act.wait_ge(ya_mm, n - 1)
                if len(CHUNKS[k % QPB]) == 4:
                    act.activation(rowsT[:, k % 2, :, :], p_tr[:, 0:2, :], ACT.Copy).then_inc(trE_done, 1)
                else:
                    act.activation(rowsT[:, k % 2, 0, :], p_tr[:, 0, :], ACT.Copy)
                    act.activation(rowsT[0:D, k % 2, 1, :], p_tr[0:D, 1, :], ACT.Copy).then_inc(trE_done, 1)

            def square_rows(t, k, n):
                m = len(CHUNKS[k % QPB])
                act.wait_ge(ya_mm, n + 1)
                if real(n - 2):
                    act.wait_ge(va_done, n - 1)
                act.activation(sqa[:, k % 2, 0:m, :], p_ya[k % 2][:, 0:m, :], ACT.Square).then_inc(sqa_done, 1)

            def square_fields(t, k, n):
                act.wait_ge(yb_done, n + 1)
                if real(n - 2):
                    act.wait_ge(vb_done, n - 1)
                act.activation(sqb[:, k % 2, :, :], yb[:, k % 2, :, :], ACT.Square).then_inc(sqb_done, 1)

            def normalise_rows(t, k, n):
                m = len(CHUNKS[k % QPB])
                act.wait_ge(va_done, n + 1)
                act.activation(sda[:, k % 2, 0:m], va[:, k % 2, 0:m], ACT.Sqrt, bias=eps[:, 0:1],
                               scale=1.0 / E).then_inc(sda_done, 1)
                act.wait_ge(ra_done, n + 1)
                if real(n - 4):
                    act.wait_ge(yb_mm, n - 2)
                for i in range(m):
                    last = act.activation(ya[:, k % 4, i, :], p_ya[k % 2][:, i, :], ACT.Copy,
                                          scale=ra[:, k % 2, i:i + 1])
                last.then_inc(ya_done, 1)

            def deviation_fields(t, k, n):
                act.wait_ge(vb_done, n + 1)
                act.activation(sdb[:, k % 2, :], vb[:, k % 2, :], ACT.Sqrt, bias=eps[:, 0:1],
                               scale=1.0 / PR).then_inc(sdb_done, 1)

            def evacuate_gram(n, par_):
                act.wait_ge(gram_mm, n + 1)
                if real(n - 2):
                    act.wait_ge(z_stored[par_], 8 * (n - par_))
                act.activation(zs[:, par_, :, :], p_z[:, :, :], ACT.Copy).then_inc(zs_done, 1)

            def back(u, k):
                if k == 1:
                    act.wait_ge(ztr_mm, u + 1)
                    act.activation(zT[:, 0:4, :], p_m[0][:, :, :], ACT.Copy)
                    act.activation(zT[:, 4, :], p_m[1][:, 0, :], ACT.Copy).then_inc(zT_done, 1)
                if k == 3:
                    act.wait_ge(lin_mm, u + 1)
                    act.activation(sqc[:, :], p_m[0][:, :, :], ACT.Square, accum_out=vc[:, 0:1]).then_inc(sqc_done, 1)
                    act.wait_ge(sqc_done, u + 1)
                    act.activation(sdc[:, :], vc[:, :], ACT.Sqrt, bias=eps[:, 0:1],
                                   scale=1.0 / MAXD).then_inc(sdc_done, 1)
                    act.wait_ge(rc_done, u + 1)
                    act.activation(on[:, :], p_m[0][:, 0:KEPT // P, :], ACT.Copy,
                                   scale=rc[:, 0:1]).then_inc(on_done, 1)
                if k == 5:
                    act.wait_ge(h1_mm, u + 1)
                    for m in range(H1 // P):
                        last = act.activation(h1[:, m, :], p_m[0][:, m, :], ACT.Relu, bias=col("b1", m))
                    last.then_inc(h1_done, 1)
                if k == 6:
                    act.wait_ge(h2_mm, u + 1)
                    for m in range(H2 // P):
                        last = act.activation(h2[:, m, :], p_m[1][:, m, :], ACT.Relu, bias=col("b2", m))
                    last.then_inc(h2_done, 1)

            def iteration(t):
                for k in range(QPT):
                    n = QPT * t + k
                    if has(n):
                        evacuate_rows(t, k, n)
                    if has(n - 1):
                        square_rows(t, k - 1, n - 1)
                    if has(n - 2):
                        square_fields(t, k - 2, n - 2)
                    if has(n - 1):
                        normalise_rows(t, k - 1, n - 1)
                    if has(n - 2):
                        deviation_fields(t, k - 2, n - 2)
                    if (found := blocks_at(t, k, 10)):
                        evacuate_gram(*found)
                    if back_at(t) is not None:
                        back(back_at(t), k)

            act.wait_ge(x_mm, 1)
            act.activation(xsq[:, :, :], p_m[0][:, :, :], ACT.Square).then_inc(x_sq, 1)
            act.wait_ge(x_var, 1)
            act.wait_ge(zeroed, 2)
            act.activation(xv[:, 1, :], xv[:, 0, :], ACT.Sqrt, bias=eps[:, 0:1], scale=1.0 / E).then_inc(x_sd, 1)
            through(act, iteration)

        @block.vector
        def _(dve):
            def sum_rows(t, k, n):
                m = len(CHUNKS[k % QPB])
                dve.wait_ge(sqa_done, n + 1)
                dve.tensor_reduce(va[:, k % 2, 0:m], sqa[:, k % 2, 0:m, :], AX.X, ALU.add).then_inc(va_done, 1)

            def scale_rows(t, k, n):
                m = len(CHUNKS[k % QPB])
                dve.wait_ge(sda_done, n + 1)
                if real(n - 2):
                    dve.wait_ge(ya_done, n - 1)
                dve.reciprocal(ra[:, k % 2, 0:m], sda[:, k % 2, 0:m]).then_inc(ra_done, 1)

            def affine_fields(t, k, n):
                dve.wait_ge(yb_mm, n + 1)
                if real(n - 2):
                    dve.wait_ge(t_done, n - 1)
                    dve.wait_ge(sqb_done, n - 1)
                dve.scalar_tensor_tensor(
                    out=yb[:, k % 2, :, :], in0=p_yb[k % 2][:, :, :], scalar=col("gs"),
                    in1=bw[:, None, :].to_broadcast([P, QB, PR]), op0=ALU.mult, op1=ALU.add,
                ).then_inc(yb_done, 1)

            def sum_fields(t, k, n):
                dve.wait_ge(sqb_done, n + 1)
                dve.tensor_reduce(vb[:, k % 2, :], sqb[:, k % 2, :, :], AX.X, ALU.add).then_inc(vb_done, 1)

            def scale_fields(t, k, n):
                dve.wait_ge(sdb_done, n + 1)
                dve.reciprocal(rb[:, k % 2, :], sdb[:, k % 2, :]).then_inc(rb_done, 1)
                dve.wait_ge(rb_done, n + 1)
                half, q = (k // QPB) % 2, k % QPB
                if q == 0 and real(n - 2 * QPB):
                    blk = 2 * t + (k // QPB)
                    dve.wait_ge(gram_mm, blk - 1)
                dve.tensor_tensor(tt[:, half, QB * q:QB * (q + 1), 1:PR + 1], yb[:, k % 2, :, :],
                                  rb[:, k % 2, :, None].to_broadcast([P, QB, PR]), ALU.mult).then_inc(t_done, 1)

            def affine_t(t, n, par_, piece):
                if piece == 0:
                    dve.wait_ge(t_done, QPB * (n + 1))
                    dve.tensor_copy(tt[:, par_, :, 0], xT[:, bass.ds(BLK * n, BLK)]).then_inc(x_put, 1)
                for p in range(11 * piece, min(11 * (piece + 1), PR)):
                    v = tt[:, par_, :, 1 + p]
                    last = dve.tensor_scalar(v, v, col("gsi", p), col("bsi", p), ALU.mult, ALU.add)
                if piece == 2:
                    last.then_inc(aff_done, 1)

            def back(u, k):
                if k == 0:
                    dve.wait_ge(z_in, 16 * (u + 1))
                    if real(u - 1):
                        dve.wait_ge(ztr_mm, u)
                    for j in range(3):
                        v = tri(j)
                        to = zp[:, j, :]
                        dims = [n for _, n in TRI[j][1]]
                        if len(dims) == 3:
                            to = to.rearrange("p (a b c) -> p a b c", a=dims[0], b=dims[1])
                        else:
                            to = to.rearrange("p (a b) -> p a b", a=dims[0])
                        last = dve.tensor_copy(to, v)
                    last.then_inc(zp_done, 1)
                if k == 3:
                    dve.wait_ge(sdc_done, u + 1)
                    dve.reciprocal(rc[:, :], sdc[:, :]).then_inc(rc_done, 1)
                if k == 4:
                    dve.wait_ge(otr_mm, u + 1)
                    for j in range(KEPT // P):
                        last = dve.tensor_scalar(oT[:, j, :], p_m[1][:, j, :], col("gl", j), col("bl", j),
                                                 ALU.mult, ALU.add)
                    last.then_inc(oT_done, 1)
                if k == 7:
                    dve.wait_ge(y_mm, u + 1)
                    dve.tensor_copy(ys[:, bass.ds(P * u, P)], p_m[0][0:1, 0, :]).then_inc(y_done, 1)

            def iteration(t):
                for k in range(QPT):
                    n = QPT * t + k
                    if has(n - 2):
                        affine_fields(t, k - 2, n - 2)
                    if has(n - 1):
                        sum_rows(t, k - 1, n - 1)
                        scale_rows(t, k - 1, n - 1)
                    if has(n - 2):
                        sum_fields(t, k - 2, n - 2)
                    for piece in range(3):
                        if (found := blocks_at(t, k, 6 + piece)):
                            affine_t(t, *found, piece)
                    if has(n - 2):
                        scale_fields(t, k - 2, n - 2)
                    if back_at(t) is not None:
                        back(back_at(t), k)

            def centre(view, n, over, done=None):
                steps[0] += 2
                dve.tensor_reduce(cen[:, 0:n], view, AX.X, ALU.add).then_inc(prep_in, 1)
                dve.wait_ge(prep_in, steps[0] - 1)
                dve.tensor_scalar(cen[:, 0:n], cen[:, 0:n], 1.0 / over, None, ALU.mult).then_inc(prep_in, 1)
                dve.wait_ge(prep_in, steps[0])
                return dve.tensor_tensor(view, view, cen[:, 0:n, None].to_broadcast([P, n, over]), ALU.subtract)

            prep_in = sem("prep_in")
            steps = [0]
            dve.memset(rowsT[:, :, :, :], 0.0).then_inc(zeroed, 1)
            dve.memset(eps[:, :], EPS).then_inc(zeroed, 1)
            dve.wait_ge(ids_in, 32)
            dve.tensor_tensor(idx[:, :], ids_sb[:, :], offs_sb[:, :], ALU.add).then_inc(idx_done, 1)

            dve.wait_ge(par_in, 16)
            dve.wait_ge(dense_in, 16)
            centre(dense_sb[:, :, 0:P], 2, P).then_inc(prep, 1)
            dve.wait_ge(prep, 1)
            wsi = col("wsi", 0, CPB * PR).rearrange("p (c r) -> p c r", r=PR)
            centre(wsi, CPB, PR).then_inc(prep_in, 1)
            steps[0] += 1
            dve.wait_ge(prep_in, steps[0])
            dve.tensor_scalar(wk[:, :], wsi[:, 0, :], col("mask"), None, ALU.mult).then_inc(prep, 1)
            centre(col("ws", 0, 2 * P).rearrange("p (g e) -> p g e", g=2), 2, P).then_inc(ws_done, 1)
            for c in range(CPB):
                m = BDCOL[c + 1] - BDCOL[c]
                v = bd[:, BDCOL[c] * PR:BDCOL[c + 1] * PR].rearrange("p (b r) -> p b r", r=PR)
                last = dve.tensor_tensor(v, wsi[:, c, None, :].to_broadcast([P, m, PR]),
                                         col("mask", BDCOL[c], m)[:, :, None].to_broadcast([P, m, PR]), ALU.mult)
            last.then_inc(bd_done, 1)
            dve.wait_ge(bw_mm, 1)
            dve.tensor_copy(bw[:, :], p_m[1][:, 0, 0:PR]).then_inc(bw_done, 1)
            dve.wait_ge(x_sq, 1)
            dve.tensor_reduce(xv[:, 0, :], xsq[:, :, :], AX.X, ALU.add).then_inc(x_var, 1)
            dve.wait_ge(x_sd, 1)
            steps[0] += 1
            dve.reciprocal(xv[:, 2, :], xv[:, 1, :]).then_inc(prep_in, 1)
            dve.wait_ge(prep_in, steps[0])
            dve.tensor_tensor(xn[:, :, :], p_m[0][:, :, :], xv[:, 2, :, None].to_broadcast([P, NT, P]),
                              ALU.mult).then_inc(x_n, 1)
            dve.wait_ge(x_tr, 1)
            dve.tensor_scalar(xT[:, :], p_m[1][:, :, :], col("gd"), col("bd"), ALU.mult, ALU.add).then_inc(x_done, 1)
            dve.wait_ge(wl_in, 16)
            dve.wait_ge(ws_done, 1)
            centre(wl[:, :, :], NK, MAXD).then_inc(wl_done, 1)
            dve.wait_ge(x_done, 1)
            dve.wait_ge(bw_done, 1)
            through(dve, iteration)


def layout(x):
    f = np.float32
    row = np.arange(CPB * P)
    field = (row % NF).reshape(CPB, P)
    off = np.cumsum([0] + VOCAB)[:NF].astype(np.int32)
    offs = np.tile(off, B).reshape(NT * CPT, P).T
    ids = np.asarray(x["ids"]).reshape(NT * CPT, P).T
    table = np.concatenate([np.asarray(x[f"tbl_{i}"]) for i in range(NF)], axis=0)
    mask = np.zeros((P, NCOL), f)
    for c, (a, b) in enumerate(SPAN):
        sample = (P * c + np.arange(P)) // NF
        for s in range(a, b):
            mask[:, BDCOL[c] + s - a] = sample == s
    wsT = np.zeros((P, 2, P), f)
    wst = np.asarray(x["L0_rec_Ws"]).T
    wsT[:D, 0], wsT[D:, 1] = wst, wst
    wsiT = np.asarray(x["L0_rec_Wsi"]).T
    columns = {
        "gs": np.asarray(x["L0_rec_gs"])[:, None], "gd": np.asarray(x["L0_rec_gd"])[:, None],
        "bd": np.asarray(x["L0_rec_bd"])[:, None],
        "gl": np.asarray(x["L0_rec_gl"])[:KEPT].reshape(-1, P).T,
        "bl": np.asarray(x["L0_rec_bl"])[:KEPT].reshape(-1, P).T,
        "b1": np.asarray(x["b_top1"]).reshape(-1, P).T, "b2": np.asarray(x["b_top2"]).reshape(-1, P).T,
        "w3": np.asarray(x["W_top3"])[:, 0].reshape(-1, P).T,
        "gsi": np.broadcast_to(np.asarray(x["L0_rec_gsi"]), (P, PR)),
        "bsi": np.broadcast_to(np.asarray(x["L0_rec_bsi"]), (P, PR)),
        "bs": np.broadcast_to(np.asarray(x["L0_rec_bs"]), (P, P)),
        "ident": np.eye(P, dtype=f), "mask": mask,
        "wsi": wsiT[field].transpose(1, 0, 2).reshape(P, CPB * PR), "ws": wsT.reshape(P, 2 * P),
    }
    params = np.concatenate([columns[k] for k in COLS], axis=1)
    wd = np.asarray(x["L0_rec_Wd"]).T.reshape(2, P, P)
    de = np.asarray(x["r_dense_t"]).T.reshape(2, P, B)
    dense = np.concatenate([wd, de], axis=2).transpose(1, 0, 2)
    wlT = np.asarray(x["L0_rec_Wl"]).T
    wlin = np.zeros((NK * P, MAXD), f)
    for r, (i, j) in enumerate(tri_pairs()):
        if j <= i:
            wlin[r] = wlT[i * (i + 1) // 2 + j]
    w1 = np.asarray(x["W_top1"])
    w1 = np.concatenate([w1[:KEPT], w1[MAXD:]], axis=0)
    return {
        "ids": ids, "offs": offs, "table": table, "params": params, "dense": dense,
        "wlin": wlin.reshape(NK, P, MAXD).transpose(1, 0, 2),
        "w1": w1.reshape(-1, P, H1).transpose(1, 0, 2),
        "w2": np.asarray(x["W_top2"]).reshape(-1, P, H2).transpose(1, 0, 2),
    }


def kernel(**inputs):
    import concourse.bacc as bacc
    from concourse.bass_utils import run_bass_kernel_spmd

    nc = bacc.Bacc("TRN2", target_bir_lowering=False, num_devices=1)
    arrays, args = {}, []
    for name, a in layout(inputs).items():
        a = np.ascontiguousarray(a)
        arrays[f"in_{name}"] = a
        args.append(nc.dram_tensor(f"in_{name}", a.shape, mybir.dt.from_np(a.dtype), kind="ExternalInput").ap())
    args.append(nc.dram_tensor("out_y", (B, 1), F32, kind="ExternalOutput").ap())
    dlrm(nc, *args)
    r = run_bass_kernel_spmd(nc, [arrays], core_ids=[0])
    return r.results[0]["out_y"]
```

```python
from contextlib import ExitStack

import numpy as np

import concourse.bass as bass
from concourse import mybir

F32 = mybir.dt.float32
I32 = mybir.dt.int32
ALU = mybir.AluOpType
ACT = mybir.ActivationFunctionType
AX = mybir.AxisListType

P = 128
VOCAB = [12500, 12500, 1250, 1000, 125000, 1000, 125000, 1000, 12500, 1250, 12500, 12500, 12500,
         1250, 12500, 125000, 12500, 1000, 1250, 1250, 1250, 1000, 1000, 1000, 1000, 1000]
B = 512
NF = len(VOCAB)
D = 64
E = 128
PR = 32
DD = 256
KEPT = 384
MAXD = 512
H1, H2 = 512, 256
EPS = 1e-5

BLK = 64
NBLK = B // BLK
QB = 16
QPB = BLK // QB
QPT = 2 * QPB
NT = B // P
NQ = NT * QPT
CPB = BLK * NF // P
CPT = 2 * CPB
assert CPB * P == BLK * NF

LAST = [-(-(QB * (q + 1) * NF) // P) - 1 for q in range(QPB)]
CHUNKS = [list(range(LAST[q - 1] + 1 if q else 0, LAST[q] + 1)) for q in range(QPB)]
SPAN = [(P * c // NF, -(-(P * (c + 1)) // NF)) for c in range(CPB)]
BDCOL = np.cumsum([0] + [b - a for a, b in SPAN]).tolist()
NCOL = BDCOL[-1]

GC = PR + 1
TRI = [sum(4 * (4 * k + 4) for k in range(g)) for g in range(PR // 4 + 1)]
HS = TRI[-1]
NEXT = PR + 2
NK = -(-(HS + NEXT) // P)
EXT = HS % P
assert HS // P == NK - 1 and EXT % 32 == 0

LAG_A, LAG_AN, LAG_B, LAG_BS, LAG_BN, LAG_G, LAG_L = 1, 2, 3, 4, 5, 6, 15
PHASES = QPT + 1

COLS = {}
NPAR = 0
for _name, _n in [("gs", 1), ("gd", 1), ("bd", 1), ("gl", KEPT // P), ("bl", KEPT // P),
                  ("b1", H1 // P), ("b2", H2 // P), ("w3", H2 // P), ("pair", 4 * NK), ("ext", 1),
                  ("mi", NK * NEXT), ("mj", NK * NEXT), ("bs", P), ("ident", P), ("mask", NCOL), ("wsi", CPB * PR), ("ws", 2 * P)]:
    COLS[_name] = (NPAR, _n)
    NPAR += _n


def pairs():
    out = []
    for g in range(PR // 4):
        out += [(i, j) if j <= i else None for i in range(4 * g, 4 * g + 4) for j in range(4 * g + 4)]
    return out + [None] * (NK * P - len(out))


def real(n):
    return not isinstance(n, int) or n >= 0


def dlrm(nc, ids, table, params, dense, wlin, w1, w2, out):
    with ExitStack() as ctx:
        def sb(name, shape, dt=F32):
            return ctx.enter_context(nc.sbuf_tensor(name, shape, dt))

        def sem(name):
            return ctx.enter_context(nc.semaphore(name))

        ids_sb = sb("ids_sb", [P, 2, NT * CPT], I32)
        idx = sb("idx", [P, NT * CPT], I32)
        par = sb("par", [P, NPAR])
        dense_sb = sb("dense_sb", [P, 2, P + B])
        wl = sb("wl", [P, NK, MAXD])
        w1s = sb("w1s", [P, (KEPT + DD) // P, H1])
        w2s = sb("w2s", [P, H1 // P, H2])
        eps = sb("eps", [P, 1])
        bd = sb("bd", [P, NCOL * PR])
        rows = sb("rows", [P, CPT, D])
        rowsT = sb("rowsT", [P, 2, 2, P])
        sqa = sb("sqa", [P, 2, 4, P])
        va = sb("va", [P, 2, 4])
        sda = sb("sda", [P, 2, 4])
        ra = sb("ra", [P, 2, 4])
        ya = sb("ya", [P, 4, 4, P])
        bw = sb("bw", [P, PR])
        yb = sb("yb", [P, 4, QB, PR])
        sqb = sb("sqb", [P, 2, QB, PR])
        vb = sb("vb", [P, 2, QB])
        sdb = sb("sdb", [P, 2, QB])
        rb = sb("rb", [P, 2, QB])
        tt = sb("tt", [P, 2, BLK, PR + 2])
        xT = sb("xT", [P, B])
        xs = sb("xs", [P, NT])
        zs = sb("zs", [P, 2, BLK // 8, GC])
        zr = sb("zr", [P, PR, GC])
        zp = sb("zp", [P, NK * P])
        zT = sb("zT", [P, NK, P])
        sqc = sb("sqc", [P, MAXD])
        vc = sb("vc", [P, 1])
        sdc = sb("sdc", [P, 1])
        rc = sb("rc", [P, 1])
        on = sb("on", [P, KEPT])
        oT = sb("oT", [P, KEPT // P, P])
        hd = sb("hd", [P, H1 // P, B])
        h1p = sb("h1p", [P, H1 // P, P])
        h1 = sb("h1", [P, H1 // P, P])
        h2 = sb("h2", [P, H2 // P, P])
        ys = sb("ys", [1, B])
        ext = sb("ext", [P, NK, NEXT])
        ext2 = sb("ext2", [P, NK, NEXT])
        ones = sb("ones", [P, 1])
        cen = sb("cen", [P, 32])
        xsq = sb("xsq", [P, NT, P])
        xv = sb("xv", [P, 3, NT])
        wm = sb("wm", [P, 2, NK])
        xn = sb("xn", [P, NT, P])
        wk = sb("wk", [P, PR])

        p_tr = ctx.enter_context(nc.psum_tensor("p_tr", [P, 4, P], F32))
        p_ya = [ctx.enter_context(nc.psum_tensor(f"p_ya{i}", [P, 4, P], F32)) for i in range(2)]
        p_yb = [ctx.enter_context(nc.psum_tensor(f"p_yb{i}", [P, QB, PR], F32)) for i in range(2)]
        p_z = ctx.enter_context(nc.psum_tensor("p_z", [P, BLK // 8, GC], F32))
        p_m = [ctx.enter_context(nc.psum_tensor(f"p_m{i}", [P, 4, P], F32)) for i in range(2)]
        zdram = nc.dram_tensor("zdram", [NT, P, PR * GC], F32, kind="Internal").ap()

        ids_in = sem("ids_in")
        par_in = sem("par_in")
        dense_in = sem("dense_in")
        wl_in = sem("wl_in")
        w1_in = sem("w1_in")
        w1d_in = sem("w1d_in")
        w2_in = sem("w2_in")
        idx_done = sem("idx_done")
        gathered = [sem(f"gathered{k}") for k in range(QPT)]
        zeroed = sem("zeroed")
        prep = sem("prep")
        ws_done = sem("ws_done")
        bd_done = sem("bd_done")
        bw_mm = sem("bw_mm")
        bw_done = sem("bw_done")
        ext_done = sem("ext_done")
        ext_mm = sem("ext_mm")
        wl_done = sem("wl_done")
        xs_mm = sem("xs_mm")
        xs_done = sem("xs_done")
        lin_step = sem("lin_step")
        hd_mm = sem("hd_mm")
        hd_done = sem("hd_done")
        x_r = sem("x_r")
        x_mm = sem("x_mm")
        x_sq = sem("x_sq")
        x_var = sem("x_var")
        x_sd = sem("x_sd")
        x_n = sem("x_n")
        x_tr = sem("x_tr")
        x_done = sem("x_done")
        tr_done = sem("tr_done")
        trE_done = sem("trE_done")
        ya_mm = sem("ya_mm")
        sqa_done = sem("sqa_done")
        va_done = sem("va_done")
        sda_done = sem("sda_done")
        ra_done = sem("ra_done")
        ya_done = sem("ya_done")
        yb_mm = sem("yb_mm")
        yb_done = sem("yb_done")
        sqb_done = sem("sqb_done")
        vb_done = sem("vb_done")
        sdb_done = sem("sdb_done")
        rb_done = sem("rb_done")
        t_done = sem("t_done")
        gram_mm = sem("gram_mm")
        x_put = sem("x_put")
        zs_done = sem("zs_done")
        z_stored = [sem(f"z_stored{i}") for i in range(2)]
        z_in = sem("z_in")
        zp_done = sem("zp_done")
        ztr_mm = sem("ztr_mm")
        zT_done = sem("zT_done")
        lin_mm = sem("lin_mm")
        sqc_done = sem("sqc_done")
        sdc_done = sem("sdc_done")
        rc_done = sem("rc_done")
        on_done = sem("on_done")
        otr_mm = sem("otr_mm")
        oT_done = sem("oT_done")
        h1_mm = sem("h1_mm")
        h1p_done = sem("h1p_done")
        h1_done = sem("h1_done")
        h2_mm = sem("h2_mm")
        h2_done = sem("h2_done")
        y_mm = sem("y_mm")
        y_done = sem("y_done")
        y_out = sem("y_out")

        def col(name, i=0, n=1):
            a = COLS[name][0] + i
            return par[:, a:a + n]

        ident = col("ident", 0, P)
        ws = [col("ws", P * g, P) for g in range(2)]

        def has(n):
            return real(n) and (not isinstance(n, int) or n < NQ)

        def through(eng, iteration):
            iteration(0)
            iteration(1)
            with eng.Fori(2, NT) as t:
                iteration(t)
            iteration(NT)
            iteration(NT + 1)

        def phases_at(t, k):
            at = []
            for phase in reversed(range(PHASES)):
                if (k - LAG_L - phase) % QPT == 0:
                    u = t + (k - LAG_L - phase) // QPT
                    if real(u) and (not isinstance(u, int) or u < NT):
                        at.append((u, phase))
            return at

        block = ctx.enter_context(nc.Block())

        @block.sync
        def _(sp):
            sp.dma_start(ids_sb[:, :, :], ids).then_inc(ids_in, 16)
            sp.dma_start(par[:, :], params).then_inc(par_in, 16)
            for k in range(5):
                sp.wait_ge(gathered[k], 16 * len(CHUNKS[k % QPB]))
                if k == 0:
                    sp.dma_start(dense_sb[:, :, :], dense).then_inc(dense_in, 16)
                for j in {0: [0, 1], 1: [2, 3], 2: [4]}.get(k, []):
                    sp.dma_start(wl[:, j, :], wlin[:, j, :]).then_inc(wl_in, 16)
                for j in {1: [3], 2: [4], 3: [0, 1, 2]}.get(k, []):
                    sp.dma_start(w1s[:, j, :], w1[:, j, :]).then_inc(w1_in if j < 3 else w1d_in, 16)
                if k == 4:
                    sp.dma_start(w2s[:, :, :], w2).then_inc(w2_in, 16)

            def tile(t):
                for half in range(4):
                    sp.wait_ge(zs_done, 4 * t + half + 1)
                    dst = zdram[t, half * 32:(half + 1) * 32, :].rearrange(
                        "(b q) (i j) -> (q i) b j", q=4, j=GC)
                    sp.dma_start(dst, zs[:, half % 2, :, :]).then_inc(z_stored[half % 2], 16)
                for half in range(2):
                    sp.wait_ge(z_stored[half], 32 * (t + 1))
                if not isinstance(t, int) or t:
                    sp.wait_ge(zp_done, t)
                sp.dma_start(zr[:, :, :], zdram[t].rearrange("b (i j) -> b i j", j=GC)).then_inc(z_in, 16)

            tile(0)
            with sp.Fori(1, NT) as t:
                tile(t)
            sp.wait_ge(y_done, NT)
            sp.dma_start(out.rearrange("b o -> o b"), ys[:, :]).then_inc(y_out, 16)
            sp.wait_ge(y_out, 16)

        @block.gpsimd
        def _(pool):
            pool.wait_ge(idx_done, 1)
            for t in range(NT):
                for k in range(QPT):
                    if t:
                        pool.wait_ge(tr_done, QPT * (t - 1) + k + 1)
                    for c in CHUNKS[k % QPB]:
                        j = CPB * (k // QPB) + c
                        pool.indirect_dma_start(
                            rows[:, j, :], None, table,
                            bass.IndirectOffsetOnAxis(ap=idx[:, CPT * t + j:CPT * t + j + 1], axis=0),
                        ).then_inc(gathered[k], 16)

        @block.tensor
        def _(pe):
            def transposes(t, k):
                n = QPT * t + k
                pe.wait_ge(gathered[k], (t + 1) * (16 * len(CHUNKS[k % QPB])))
                if real(n - 1):
                    pe.wait_ge(trE_done, n)
                ch = [CPB * (k // QPB) + c for c in CHUNKS[k % QPB]]
                for u in range(2):
                    two = len(ch) > 2 * u + 1
                    src = rows[:, ch[2 * u]:ch[2 * u] + (2 if two else 1), :].rearrange("p c d -> p (c d)")
                    last = pe.transpose(p_tr[0:D * (2 if two else 1), u, :], src, ident)
                last.then_inc(tr_done, 1)

            def project_rows(t, k, n):
                if isinstance(n, int) and n == 0:
                    pe.wait_ge(ws_done, 1)
                pe.wait_ge(trE_done, n + 1)
                if real(n - 2):
                    pe.wait_ge(ya_done, n - 1)
                for i, c in enumerate(CHUNKS[k % QPB]):
                    last = pe.matmul(p_ya[k % 2][:, i, :], rowsT[:, k % 2, i // 2, :], ws[i % 2],
                                     start=True, stop=True)
                last.then_inc(ya_mm, 1)

            def project_fields(t, k, n):
                if isinstance(n, int) and n == 0:
                    pe.wait_ge(bd_done, 1)
                pe.wait_ge(ya_done, n + 1)
                if real(n - 2):
                    pe.wait_ge(yb_done, n - 1)
                q = k % QPB
                lo, hi = QB * q, QB * (q + 1)
                parts = [c for c in range(CPB) if SPAN[c][0] < hi and SPAN[c][1] > lo and c <= LAST[q]]
                for c in parts:
                    a, b = max(SPAN[c][0], lo), min(SPAN[c][1], hi)
                    own = c in CHUNKS[q]
                    kk = k if own else k - 1
                    i = CHUNKS[q].index(c) if own else CHUNKS[q - 1].index(c)
                    r = (BDCOL[c] + a - SPAN[c][0]) * PR
                    last = pe.matmul(p_yb[k % 2][:, a - lo:b - lo, :], ya[:, kk % 4, i, :],
                                     bd[:, r:r + (b - a) * PR], start=(c == parts[0]),
                                     stop=(c == parts[-1]), skip_group_check=True)
                last.then_inc(yb_mm, 1)

            def gram(t, k, n):
                pe.wait_ge(t_done, n + 1)
                if k % 2 == 0 and real(n - 2):
                    pe.wait_ge(zs_done, (4 * t + k // 2))
                q = k % QPB
                for b in range(QB * q, QB * (q + 1)):
                    last = pe.matmul(p_z[PR * (b % 4):PR * (b % 4 + 1), b % 32 // 4, :],
                                     tt[:, k // QPB % 2, b, 2:PR + 2], tt[:, k // QPB % 2, b, 0:GC],
                                     start=True, stop=True)
                last.then_inc(gram_mm, 1)

            def back(u, k):
                if k == 1:
                    pe.wait_ge(zp_done, u + 1)
                    if real(u - 1):
                        pe.wait_ge(y_done, u)
                    for j in range(NK):
                        last = pe.transpose(p_m[j // 4][:, j % 4, :], zp[:, P * j:P * (j + 1)], ident)
                    last.then_inc(ztr_mm, 1)
                if k in (2, 3):
                    if k == 2:
                        pe.wait_ge(zT_done, u + 1)
                        if isinstance(u, int) and u == 0:
                            pe.wait_ge(wl_done, 1)
                    m = slice(2 * (k - 2), 2 * (k - 1))
                    for j in range(NK):
                        last = pe.matmul(p_m[0][:, m, :], zT[:, j, :], wl[:, j, 256 * (k - 2):256 * (k - 1)],
                                         start=(j == 0), stop=(j == NK - 1))
                    last.then_inc(lin_mm, 1)
                if k == 4:
                    pe.wait_ge(on_done, u + 1)
                    for j in range(KEPT // P):
                        last = pe.transpose(p_m[1][:, j, :], on[:, P * j:P * (j + 1)], ident)
                    last.then_inc(otr_mm, 1)
                if k in (5, 6):
                    if k == 5:
                        pe.wait_ge(oT_done, u + 1)
                    for m in (2 * (k - 5), 2 * (k - 5) + 1):
                        for j in range(KEPT // P):
                            last = pe.matmul(p_m[0][:, m, :], w1s[:, j, P * m:P * (m + 1)], oT[:, j, :],
                                             start=(j == 0), stop=(j == KEPT // P - 1))
                    if k == 6:
                        last.then_inc(h1_mm, 1)
                if k == 7:
                    pe.wait_ge(h1_done, u + 1)
                    for m in range(H2 // P):
                        for j in range(H1 // P):
                            last = pe.matmul(p_m[1][:, m, :], w2s[:, j, P * m:P * (m + 1)], h1[:, j, :],
                                             start=(j == 0), stop=(j == H1 // P - 1))
                    last.then_inc(h2_mm, 1)
                if k == 8:
                    pe.wait_ge(h2_done, u + 1)
                    for j in range(H2 // P):
                        last = pe.matmul(p_m[0][0:1, 0, :], col("w3", j), h2[:, j, :],
                                         start=(j == 0), stop=(j == H2 // P - 1))
                    last.then_inc(y_mm, 1)

            def first_steps(n):
                if n == 1:
                    pe.wait_ge(prep, 2)
                    for t in range(NT):
                        for j in range(2):
                            last = pe.matmul(p_m[0][:, t, :], dense_sb[:, j, P + P * t:P + P * (t + 1)],
                                             dense_sb[:, j, 0:P], start=(j == 0), stop=(j == 1))
                    last.then_inc(x_mm, 1)
                    pe.matmul(p_m[1][:, 0, 0:PR], col("bs", 0, P), wk[:, :], start=True,
                              stop=True).then_inc(bw_mm, 1)
                if n == 2:
                    pe.wait_ge(bw_done, 1)
                    pe.wait_ge(x_n, 1)
                    for t in range(NT):
                        last = pe.transpose(p_m[1][:, t, :], xn[:, t, :], ident)
                    last.then_inc(x_tr, 1)
                if n == 3:
                    pe.wait_ge(x_done, 1)
                    for t in range(NT):
                        last = pe.matmul(p_m[1][:, 0, t:t + 1], xT[:, P * t:P * (t + 1)], ones[:, :],
                                         start=True, stop=True)
                    last.then_inc(xs_mm, 1)
                if 4 <= n < 4 + H1 // P:
                    m = n - 4
                    if m == 0:
                        pe.wait_ge(w1d_in, 32)
                        pe.wait_ge(x_n, 1)
                    if m == 1:
                        pe.wait_ge(xs_done, 1)
                    if m >= 2:
                        pe.wait_ge(hd_done, m - 1)
                    for j in range(2):
                        last = pe.matmul(p_m[m % 2][:, :, :], w1s[:, KEPT // P + j, P * m:P * (m + 1)],
                                         dense_sb[:, j, P:P + B], start=(j == 0), stop=(j == 1))
                    last.then_inc(hd_mm, 1)
                if n == 10:
                    pe.wait_ge(ext_done, 1)
                    pe.wait_ge(hd_done, 3)
                    for j in range(NK):
                        last = pe.matmul(p_m[0][EXT:EXT + NEXT, :, :], ext[:, j, :], wl[:, j, :],
                                         start=(j == 0), stop=(j == NK - 1))
                    last.then_inc(ext_mm, 1)
                if n == 12:
                    pe.wait_ge(w1_in, 48)
                    pe.wait_ge(w2_in, 16)

            def iteration(t):
                for k in range(QPT):
                    n = QPT * t + k
                    if has(n - LAG_B):
                        project_fields(t, k - LAG_B, n - LAG_B)
                    if has(n - LAG_A):
                        project_rows(t, k - LAG_A, n - LAG_A)
                    if has(n):
                        transposes(t, k)
                    if has(n - LAG_G):
                        gram(t, k - LAG_G, n - LAG_G)
                    if isinstance(t, int) and n <= 12:
                        first_steps(n)
                    for u, phase in phases_at(t, k):
                        back(u, phase)

            pe.wait_ge(zeroed, 5)
            pe.wait_ge(par_in, 16)
            through(pe, iteration)

        @block.scalar
        def _(act):
            def evacuate_rows(t, k, n):
                act.wait_ge(tr_done, n + 1)
                if real(n - 2):
                    act.wait_ge(ya_mm, n - 1)
                if len(CHUNKS[k % QPB]) == 4:
                    act.activation(rowsT[:, k % 2, :, :], p_tr[:, 0:2, :], ACT.Copy).then_inc(trE_done, 1)
                else:
                    act.activation(rowsT[:, k % 2, 0, :], p_tr[:, 0, :], ACT.Copy)
                    act.activation(rowsT[0:D, k % 2, 1, :], p_tr[0:D, 1, :], ACT.Copy).then_inc(trE_done, 1)

            def square_rows(t, k, n):
                m = len(CHUNKS[k % QPB])
                act.wait_ge(ya_mm, n + 1)
                if real(n - 2):
                    act.wait_ge(va_done, n - 1)
                act.activation(sqa[:, k % 2, 0:m, :], p_ya[k % 2][:, 0:m, :], ACT.Square).then_inc(sqa_done, 1)

            def square_fields(t, k, n):
                act.wait_ge(yb_done, n + 1)
                if real(n - 2):
                    act.wait_ge(vb_done, n - 1)
                act.activation(sqb[:, k % 2, :, :], yb[:, k % 4, :, :], ACT.Square).then_inc(sqb_done, 1)

            def deviation_rows(t, k, n):
                m = len(CHUNKS[k % QPB])
                act.wait_ge(va_done, n + 1)
                act.activation(sda[:, k % 2, 0:m], va[:, k % 2, 0:m], ACT.Sqrt, bias=eps[:, 0:1],
                               scale=1.0 / E).then_inc(sda_done, 1)

            def normalise_rows(t, k, n):
                m = len(CHUNKS[k % QPB])
                act.wait_ge(ra_done, n + 1)
                if real(n - 4):
                    act.wait_ge(yb_mm, n - 2)
                for i in range(m):
                    last = act.activation(ya[:, k % 4, i, :], p_ya[k % 2][:, i, :], ACT.Copy,
                                          scale=ra[:, k % 2, i:i + 1])
                last.then_inc(ya_done, 1)

            def deviation_fields(t, k, n):
                act.wait_ge(vb_done, n + 1)
                if real(n - 2):
                    act.wait_ge(rb_done, n - 1)
                act.activation(sdb[:, k % 2, :], vb[:, k % 2, :], ACT.Sqrt, bias=eps[:, 0:1],
                               scale=1.0 / PR).then_inc(sdb_done, 1)

            def evacuate_gram(t, k, n):
                half = k // 2
                act.wait_ge(gram_mm, n + 1)
                if real(n - 4):
                    act.wait_ge(z_stored[half % 2], 16 * (2 * t + half // 2))
                act.activation(zs[:, half % 2, :, :], p_z[:, :, :], ACT.Copy).then_inc(zs_done, 1)

            def back(u, k):
                if k == 1:
                    act.wait_ge(ztr_mm, u + 1)
                    act.activation(zT[:, 0:4, :], p_m[0][:, :, :], ACT.Copy)
                    act.activation(zT[:, 4, :], p_m[1][:, 0, :], ACT.Copy).then_inc(zT_done, 1)
                if k == 3:
                    act.wait_ge(lin_mm, 2 * (u + 1))
                    act.activation(sqc[:, :], p_m[0][:, :, :], ACT.Square, accum_out=vc[:, 0:1]).then_inc(sqc_done, 1)
                    act.wait_ge(sqc_done, u + 1)
                    act.activation(sdc[:, :], vc[:, :], ACT.Sqrt, bias=eps[:, 0:1],
                                   scale=1.0 / MAXD).then_inc(sdc_done, 1)
                    act.wait_ge(rc_done, u + 1)
                    act.activation(on[:, :], p_m[0][:, 0:KEPT // P, :], ACT.Copy,
                                   scale=rc[:, 0:1]).then_inc(on_done, 1)
                if k == 6:
                    act.wait_ge(h1p_done, u + 1)
                    act.activation(h1[:, :, :], h1p[:, :, :], ACT.Relu).then_inc(h1_done, 1)
                if k == 7:
                    act.wait_ge(h2_mm, u + 1)
                    for m in range(H2 // P):
                        last = act.activation(h2[:, m, :], p_m[1][:, m, :], ACT.Relu, bias=col("b2", m))
                    last.then_inc(h2_done, 1)

            def first_steps(n):
                if n == 1:
                    act.wait_ge(x_mm, 1)
                    act.activation(xsq[:, :, :], p_m[0][:, :, :], ACT.Square).then_inc(x_sq, 1)
                    act.wait_ge(x_var, 1)
                    act.activation(xv[:, 1, :], xv[:, 0, :], ACT.Sqrt, bias=eps[:, 0:1],
                                   scale=1.0 / E).then_inc(x_sd, 1)
                if 4 <= n < 4 + H1 // P:
                    m = n - 4
                    act.wait_ge(hd_mm, m + 1)
                    act.activation(hd[:, m, :], p_m[m % 2][:, :, :], ACT.Identity,
                                   bias=col("b1", m)).then_inc(hd_done, 1)

            def iteration(t):
                for k in range(QPT):
                    n = QPT * t + k
                    if has(n - LAG_AN):
                        deviation_rows(t, k - LAG_AN, n - LAG_AN)
                    if has(n - LAG_A):
                        square_rows(t, k - LAG_A, n - LAG_A)
                    if has(n - LAG_AN):
                        normalise_rows(t, k - LAG_AN, n - LAG_AN)
                    if has(n - LAG_G) and (k - LAG_G) % 2:
                        evacuate_gram(t, k - LAG_G, n - LAG_G)
                    if has(n - LAG_BS):
                        deviation_fields(t, k - LAG_BS, n - LAG_BS)
                    if has(n - LAG_B):
                        square_fields(t, k - LAG_B, n - LAG_B)
                    if has(n):
                        evacuate_rows(t, k, n)
                    if isinstance(t, int) and n <= 12:
                        first_steps(n)
                    for u, phase in phases_at(t, k):
                        back(u, phase)

            act.wait_ge(zeroed, 2)
            act.wait_ge(par_in, 16)
            through(act, iteration)

        @block.vector
        def _(dve):
            def sum_rows(t, k, n):
                m = len(CHUNKS[k % QPB])
                dve.wait_ge(sqa_done, n + 1)
                dve.tensor_reduce(va[:, k % 2, 0:m], sqa[:, k % 2, 0:m, :], AX.X, ALU.add).then_inc(va_done, 1)

            def scale_rows(t, k, n):
                m = len(CHUNKS[k % QPB])
                dve.wait_ge(sda_done, n + 1)
                if real(n - 2):
                    dve.wait_ge(ya_done, n - 1)
                dve.reciprocal(ra[:, k % 2, 0:m], sda[:, k % 2, 0:m]).then_inc(ra_done, 1)

            def affine_fields(t, k, n):
                dve.wait_ge(yb_mm, n + 1)
                if real(n - 4):
                    dve.wait_ge(t_done, n - 3)
                dve.scalar_tensor_tensor(
                    out=yb[:, k % 4, :, :], in0=p_yb[k % 2][:, :, :], scalar=col("gs"),
                    in1=bw[:, None, :].to_broadcast([P, QB, PR]), op0=ALU.mult, op1=ALU.add,
                ).then_inc(yb_done, 1)

            def sum_fields(t, k, n):
                dve.wait_ge(sqb_done, n + 1)
                dve.tensor_reduce(vb[:, k % 2, :], sqb[:, k % 2, :, :], AX.X, ALU.add).then_inc(vb_done, 1)

            def normalise_fields(t, k, n):
                dve.wait_ge(sdb_done, n + 1)
                dve.reciprocal(rb[:, k % 2, :], sdb[:, k % 2, :]).then_inc(rb_done, 1)
                dve.wait_ge(rb_done, n + 1)
                half, q = (k // QPB) % 2, k % QPB
                if q == 0:
                    blk = 2 * t + k // QPB
                    if real(n - 2 * QPB):
                        dve.wait_ge(gram_mm, n - QPB)
                    dve.tensor_copy(tt[:, half, :, 1], xT[:, bass.ds(BLK * blk, BLK)]).then_inc(x_put, 1)
                dve.tensor_tensor(tt[:, half, QB * q:QB * (q + 1), 2:PR + 2], yb[:, k % 4, :, :],
                                  rb[:, k % 2, :, None].to_broadcast([P, QB, PR]), ALU.mult).then_inc(t_done, 1)

            def back(u, k):
                if k == 0:
                    dve.wait_ge(z_in, 16 * (u + 1))
                    if real(u - 1):
                        dve.wait_ge(ztr_mm, u)
                    for g in range(PR // 4):
                        w = 4 * g + 4
                        dve.tensor_copy(zp[:, TRI[g]:TRI[g + 1]].rearrange("p (i j) -> p i j", j=w),
                                        zr[:, 4 * g:4 * g + 4, 1:1 + w])
                    dve.tensor_copy(zp[:, HS:HS + PR], zr[:, :, 0])
                    dve.tensor_copy(zp[:, HS + PR:HS + PR + 1], xs[:, bass.ds(u, 1)]).then_inc(zp_done, 1)
                if k == 3:
                    dve.wait_ge(sdc_done, u + 1)
                    dve.reciprocal(rc[:, :], sdc[:, :]).then_inc(rc_done, 1)
                if k == 4:
                    dve.wait_ge(otr_mm, u + 1)
                    for j in range(KEPT // P):
                        last = dve.tensor_scalar(oT[:, j, :], p_m[1][:, j, :], col("gl", j), col("bl", j),
                                                 ALU.mult, ALU.add)
                    last.then_inc(oT_done, 1)
                if k == 6:
                    dve.wait_ge(h1_mm, u + 1)
                    dve.tensor_tensor(h1p[:, :, :], p_m[0][:, :, :], hd[:, :, bass.ds(P * u, P)],
                                      ALU.add).then_inc(h1p_done, 1)
                if k == 8:
                    dve.wait_ge(y_mm, u + 1)
                    dve.tensor_copy(ys[:, bass.ds(P * u, P)], p_m[0][0:1, 0, :]).then_inc(y_done, 1)

            def first_steps(n):
                if n == 1:
                    dve.wait_ge(bw_mm, 1)
                    dve.tensor_copy(bw[:, :], p_m[1][:, 0, 0:PR]).then_inc(bw_done, 1)
                    dve.wait_ge(bw_done, 1)
                    dve.wait_ge(x_sq, 1)
                    dve.tensor_reduce(xv[:, 0, :], xsq[:, :, :], AX.X, ALU.add).then_inc(x_var, 1)
                    dve.wait_ge(x_sd, 1)
                    dve.reciprocal(xv[:, 2, :], xv[:, 1, :]).then_inc(x_r, 1)
                    dve.wait_ge(x_r, 1)
                    dve.tensor_tensor(xn[:, :, :], p_m[0][:, :, :], xv[:, 2, :, None].to_broadcast([P, NT, P]),
                                      ALU.mult).then_inc(x_n, 1)
                if n == 2:
                    dve.wait_ge(x_tr, 1)
                    dve.tensor_scalar(xT[:, :], p_m[1][:, :, :], col("gd"), col("bd"), ALU.mult,
                                      ALU.add).then_inc(x_done, 1)
                if n == 3:
                    dve.wait_ge(x_done, 1)
                    dve.wait_ge(xs_mm, 1)
                    dve.tensor_copy(xs[:, :], p_m[1][:, 0, 0:NT]).then_inc(xs_done, 1)
                    dve.wait_ge(xs_done, 1)

            def iteration(t):
                for k in range(QPT):
                    n = QPT * t + k
                    if has(n - LAG_AN):
                        scale_rows(t, k - LAG_AN, n - LAG_AN)
                    if has(n - LAG_BS):
                        sum_fields(t, k - LAG_BS, n - LAG_BS)
                    if has(n - LAG_B):
                        affine_fields(t, k - LAG_B, n - LAG_B)
                    if isinstance(t, int) and n <= 3:
                        first_steps(n)
                    if isinstance(t, int) and 4 <= n <= 11:
                        prepare_linear(n - 3)
                    if has(n - LAG_A):
                        sum_rows(t, k - LAG_A, n - LAG_A)
                    if has(n - LAG_BN):
                        normalise_fields(t, k - LAG_BN, n - LAG_BN)
                    for u, phase in phases_at(t, k):
                        back(u, phase)

            def prepare_linear(n):
                if n == 1:
                    dve.wait_ge(wl_in, 16 * NK)
                if n <= 5:
                    j = n - 1
                    dve.tensor_reduce(wm[:, 0, j:j + 1], wl[:, j, :], AX.X, ALU.add).then_inc(lin_step, 1)
                    dve.wait_ge(lin_step, 3 * j + 1)
                    dve.tensor_scalar(wm[:, 1, j:j + 1], wm[:, 0, j:j + 1], 1.0 / MAXD, None,
                                      ALU.mult).then_inc(lin_step, 1)
                    dve.wait_ge(lin_step, 3 * j + 2)
                    dve.tensor_scalar(wl[:, j, :], wl[:, j, :], wm[:, 1, j:j + 1], None,
                                      ALU.subtract).then_inc(lin_step, 1)
                if n == 6:
                    pair = [col("pair", NK * i, NK) for i in range(4)]
                    mi = col("mi", 0, NK * NEXT).rearrange("p (c r) -> p c r", r=NEXT)
                    mj = col("mj", 0, NK * NEXT).rearrange("p (c r) -> p c r", r=NEXT)
                    dve.tensor_tensor(ext[:, :, :], mi, pair[1][:, :, None].to_broadcast([P, NK, NEXT]),
                                      ALU.mult).then_inc(lin_step, 1)
                    dve.tensor_tensor(ext2[:, :, :], mj, pair[0][:, :, None].to_broadcast([P, NK, NEXT]),
                                      ALU.mult).then_inc(lin_step, 1)
                    dve.wait_ge(lin_step, 17)
                    dve.tensor_tensor(ext[:, :, NEXT - 1], ext[:, :, NEXT - 1], pair[0], ALU.mult).then_inc(lin_step, 1)
                    dve.wait_ge(lin_step, 18)
                    dve.tensor_tensor(ext[:, :, :], ext[:, :, :], ext2[:, :, :], ALU.add).then_inc(ext_done, 1)
                if n == 8:
                    dve.wait_ge(ext_mm, 1)
                    for j in range(0, NK - 1):
                        dve.tensor_scalar(wl[:, j, :], wl[:, j, :], col("pair", 2 * NK + j),
                                          col("pair", 3 * NK + j), ALU.mult, ALU.mult)
                    j = NK - 1
                    dve.tensor_scalar(wl[0:EXT, j, :], wl[0:EXT, j, :], col("pair", 2 * NK + j)[0:EXT],
                                      col("pair", 3 * NK + j)[0:EXT], ALU.mult, ALU.mult)
                    dve.tensor_scalar(wl[EXT:EXT + NEXT, j, :], p_m[0][EXT:EXT + NEXT, :, :],
                                      col("ext")[EXT:EXT + NEXT], None, ALU.mult).then_inc(wl_done, 1)

            def centre(view, n, over, done=None):
                steps[0] += 2
                dve.tensor_reduce(cen[:, 0:n], view, AX.X, ALU.add).then_inc(prep_in, 1)
                dve.wait_ge(prep_in, steps[0] - 1)
                dve.tensor_scalar(cen[:, 0:n], cen[:, 0:n], 1.0 / over, None, ALU.mult).then_inc(prep_in, 1)
                dve.wait_ge(prep_in, steps[0])
                return dve.tensor_tensor(view, view, cen[:, 0:n, None].to_broadcast([P, n, over]), ALU.subtract)

            prep_in = sem("prep_in")
            steps = [0]
            dve.memset(rowsT[:, :, :, :], 0.0).then_inc(zeroed, 1)
            dve.memset(eps[:, :], EPS).then_inc(zeroed, 1)
            dve.memset(ones[:, :], 1.0).then_inc(zeroed, 1)
            dve.memset(tt[:, :, :, 0], 1.0).then_inc(zeroed, 1)
            dve.memset(zp[:, HS + PR:HS + PR + 2], 1.0)
            dve.memset(zp[:, HS + NEXT:], 0.0).then_inc(zeroed, 1)
            dve.wait_ge(ids_in, 16)
            dve.tensor_tensor(idx[:, :], ids_sb[:, 0, :], ids_sb[:, 1, :], ALU.add).then_inc(idx_done, 1)

            dve.wait_ge(par_in, 16)
            centre(col("ws", 0, 2 * P).rearrange("p (g e) -> p g e", g=2), 2, P).then_inc(ws_done, 1)
            dve.wait_ge(ws_done, 1)
            wsi = col("wsi", 0, CPB * PR).rearrange("p (c r) -> p c r", r=PR)
            centre(wsi, CPB, PR).then_inc(prep_in, 1)
            steps[0] += 1
            dve.wait_ge(prep_in, steps[0])
            dve.tensor_scalar(wk[:, :], wsi[:, 0, :], col("mask"), None, ALU.mult).then_inc(prep, 1)
            for c in range(CPB):
                m = BDCOL[c + 1] - BDCOL[c]
                v = bd[:, BDCOL[c] * PR:BDCOL[c + 1] * PR].rearrange("p (b r) -> p b r", r=PR)
                last = dve.tensor_tensor(v, wsi[:, c, None, :].to_broadcast([P, m, PR]),
                                         col("mask", BDCOL[c], m)[:, :, None].to_broadcast([P, m, PR]), ALU.mult)
            last.then_inc(bd_done, 1)
            dve.wait_ge(dense_in, 16)
            centre(dense_sb[:, :, 0:P], 2, P).then_inc(prep, 1)
            through(dve, iteration)


def layout(x):
    f = np.float32
    row = np.arange(CPB * P)
    field = (row % NF).reshape(CPB, P)
    off = np.cumsum([0] + VOCAB)[:NF].astype(np.int32)
    offs = np.tile(off, B).reshape(NT * CPT, P).T
    ids = np.asarray(x["ids"]).reshape(NT * CPT, P).T
    table = np.concatenate([np.asarray(x[f"tbl_{i}"]) for i in range(NF)], axis=0)
    mask = np.zeros((P, NCOL), f)
    for c, (a, b) in enumerate(SPAN):
        sample = (P * c + np.arange(P)) // NF
        for s in range(a, b):
            mask[:, BDCOL[c] + s - a] = sample == s
    wsT = np.zeros((P, 2, P), f)
    wst = np.asarray(x["L0_rec_Ws"]).T
    wsT[:D, 0], wsT[D:, 1] = wst, wst
    wsiT = np.asarray(x["L0_rec_Wsi"]).T
    g, o = np.asarray(x["L0_rec_gsi"]), np.asarray(x["L0_rec_bsi"])
    pair = np.zeros((P, 4, NK), f)
    mi, mj = np.zeros((NK, P, NEXT), f), np.zeros((NK, P, NEXT), f)
    for s, ij in enumerate(pairs()):
        if ij is None:
            continue
        c, r, (i, j) = s // P, s % P, ij
        pair[r, 0, c], pair[r, 2, c], pair[r, 3, c] = o[i], g[i], 1
        mj[c, r, j - 1 if j else PR] = 1
        if j:
            pair[r, 1, c], pair[r, 3, c] = o[j - 1], g[j - 1]
            mi[c, r, i], mi[c, r, NEXT - 1] = 1, E
    ext = np.zeros((P, 1), f)
    ext[EXT:EXT + NEXT, 0] = 1
    ext[EXT:EXT + PR, 0] = g
    columns = {
        "gs": np.asarray(x["L0_rec_gs"])[:, None], "gd": np.asarray(x["L0_rec_gd"])[:, None],
        "bd": np.asarray(x["L0_rec_bd"])[:, None],
        "gl": np.asarray(x["L0_rec_gl"])[:KEPT].reshape(-1, P).T,
        "bl": np.asarray(x["L0_rec_bl"])[:KEPT].reshape(-1, P).T,
        "b1": np.asarray(x["b_top1"]).reshape(-1, P).T, "b2": np.asarray(x["b_top2"]).reshape(-1, P).T,
        "w3": np.asarray(x["W_top3"])[:, 0].reshape(-1, P).T,
        "pair": pair.reshape(P, 4 * NK), "ext": ext,
        "mi": mi.transpose(1, 0, 2).reshape(P, -1), "mj": mj.transpose(1, 0, 2).reshape(P, -1),
        "bs": np.broadcast_to(np.asarray(x["L0_rec_bs"]), (P, P)),
        "ident": np.eye(P, dtype=f), "mask": mask,
        "wsi": wsiT[field].transpose(1, 0, 2).reshape(P, CPB * PR), "ws": wsT.reshape(P, 2 * P),
    }
    params = np.concatenate([columns[k] for k in COLS], axis=1)
    wd = np.asarray(x["L0_rec_Wd"]).T.reshape(2, P, P)
    de = np.asarray(x["r_dense_t"]).T.reshape(2, P, B)
    dense = np.concatenate([wd, de], axis=2).transpose(1, 0, 2)
    wlT = np.asarray(x["L0_rec_Wl"]).T
    wlin = np.zeros((NK * P, MAXD), f)
    for r, ij in enumerate(pairs()):
        if ij is not None:
            wlin[r] = wlT[ij[0] * (ij[0] + 1) // 2 + ij[1]]
    w1 = np.asarray(x["W_top1"])
    w1 = np.concatenate([w1[:KEPT], w1[MAXD:]], axis=0)
    return {
        "ids": np.stack([ids, offs], axis=1), "table": table, "params": params, "dense": dense,
        "wlin": wlin.reshape(NK, P, MAXD).transpose(1, 0, 2),
        "w1": w1.reshape(-1, P, H1).transpose(1, 0, 2),
        "w2": np.asarray(x["W_top2"]).reshape(-1, P, H2).transpose(1, 0, 2),
    }


def kernel(**inputs):
    import concourse.bacc as bacc
    from concourse.bass_utils import run_bass_kernel_spmd

    nc = bacc.Bacc("TRN2", target_bir_lowering=False, num_devices=1)
    arrays, args = {}, []
    for name, a in layout(inputs).items():
        a = np.ascontiguousarray(a)
        arrays[f"in_{name}"] = a
        args.append(nc.dram_tensor(f"in_{name}", a.shape, mybir.dt.from_np(a.dtype), kind="ExternalInput").ap())
    args.append(nc.dram_tensor("out_y", (B, 1), F32, kind="ExternalOutput").ap())
    dlrm(nc, *args)
    r = run_bass_kernel_spmd(nc, [arrays], core_ids=[0])
    return r.results[0]["out_y"]
```

```python
from contextlib import ExitStack

import numpy as np

import concourse.bass as bass
from concourse import mybir

F32 = mybir.dt.float32
I32 = mybir.dt.int32
ALU = mybir.AluOpType
ACT = mybir.ActivationFunctionType
AX = mybir.AxisListType

P = 128
VOCAB = [12500, 12500, 1250, 1000, 125000, 1000, 125000, 1000, 12500, 1250, 12500, 12500, 12500,
         1250, 12500, 125000, 12500, 1000, 1250, 1250, 1250, 1000, 1000, 1000, 1000, 1000]
B = 512
NF = len(VOCAB)
D = 64
E = 128
PR = 32
DD = 256
KEPT = 384
MAXD = 512
H1, H2 = 512, 256
EPS = 1e-5

BLK = 64
QB = 16
QPB = BLK // QB
QPT = 2 * QPB
NT = B // P
NQ = NT * QPT
CPB = BLK * NF // P
CPT = 2 * CPB
assert CPB * P == BLK * NF

LAST = [-(-(QB * (q + 1) * NF) // P) - 1 for q in range(QPB)]
CHUNKS = [list(range(LAST[q - 1] + 1 if q else 0, LAST[q] + 1)) for q in range(QPB)]
SPAN = [(P * c // NF, -(-(P * (c + 1)) // NF)) for c in range(CPB)]
BDCOL = np.cumsum([0] + [b - a for a, b in SPAN]).tolist()
NCOL = BDCOL[-1]

GC = PR + 1
TRI = [sum(4 * (4 * k + 4) for k in range(g)) for g in range(PR // 4 + 1)]
HS = TRI[-1]
NEXT = PR + 2
NK = -(-(HS + NEXT) // P)
EXT = HS % P
assert HS // P == NK - 1 and EXT % 32 == 0

LAG_A, LAG_AN, LAG_B, LAG_BS, LAG_BN, LAG_G, LAG_L = 1, 2, 3, 4, 4, 6, 15
PHASES = QPT + 1
HD = [(0, (4, 5)), (1, (6, 8)), (1, (9, 11)), (0, (12, 14))]
LIN = 8
LIN_CHUNKS = [NK - 1] + list(range(NK - 1))

COLS = {}
NPAR = 0
for _name, _n in [("gs", 1), ("gd", 1), ("bd", 1), ("gl", KEPT // P), ("bl", KEPT // P),
                  ("b1", H1 // P), ("b2", H2 // P), ("w3", H2 // P), ("pair", 4 * NK), ("ext", 1),
                  ("mi", NK * NEXT), ("mj", NK * NEXT), ("bs", P), ("ident", P), ("mask", NCOL),
                  ("wsi", CPB * PR), ("ws", 2 * P)]:
    COLS[_name] = (NPAR, _n)
    NPAR += _n


def pairs():
    out = []
    for g in range(PR // 4):
        out += [(i, j) if j <= i else None for i in range(4 * g, 4 * g + 4) for j in range(4 * g + 4)]
    return out + [None] * (NK * P - len(out))


def real(n):
    return not isinstance(n, int) or n >= 0


def dlrm(nc, ids, table, params, dense, wlin, w1, w2, out):
    with ExitStack() as ctx:
        def sb(name, shape, dt=F32):
            return ctx.enter_context(nc.sbuf_tensor(name, shape, dt))

        def sem(name):
            return ctx.enter_context(nc.semaphore(name))

        ids_sb = sb("ids_sb", [P, 2, NT * CPT], I32)
        idx = sb("idx", [P, NT * CPT], I32)
        par = sb("par", [P, NPAR])
        dense_sb = sb("dense_sb", [P, 2, P + B])
        wl = sb("wl", [P, NK, MAXD])
        w1s = sb("w1s", [P, (KEPT + DD) // P, H1])
        w2s = sb("w2s", [P, H1 // P, H2])
        eps = sb("eps", [P, 1])
        bd = sb("bd", [P, NCOL * PR])
        rows = sb("rows", [P, CPT, D])
        rowsT = sb("rowsT", [P, 2, 2, P])
        sqa = sb("sqa", [P, 2, 4, P])
        va = sb("va", [P, 2, 4])
        sda = sb("sda", [P, 2, 4])
        ra = sb("ra", [P, 2, 4])
        ya = sb("ya", [P, 4, 4, P])
        bw = sb("bw", [P, PR])
        yb = sb("yb", [P, 4, QB, PR])
        sqb = sb("sqb", [P, 2, QB, PR])
        vb = sb("vb", [P, 2, QB])
        sdb = sb("sdb", [P, 2, QB])
        rb = sb("rb", [P, 2, QB])
        tt = sb("tt", [P, 2, BLK, PR + 2])
        xT = sb("xT", [P, B])
        xs = sb("xs", [P, NT])
        zs = sb("zs", [P, 2, BLK // 8, GC])
        zr = sb("zr", [P, PR, GC])
        zp = sb("zp", [P, NK * P])
        zT = sb("zT", [P, NK, P])
        zl = sb("zl", [P, KEPT // P, P])
        sqc = sb("sqc", [P, MAXD // P, P])
        vs = sb("vs", [P, P])
        sdc = sb("sdc", [P, P])
        rc = sb("rc", [1, P])
        hd = sb("hd", [P, H1 // P, B])
        hs = sb("hs", [P, H1 // P, P])
        h1p = sb("h1p", [P, H1 // P, P])
        h2p = sb("h2p", [P, H2 // P, P])
        b1 = sb("b1", [P, H1 // P])
        h1 = sb("h1", [P, H1 // P, P])
        h2 = sb("h2", [P, H2 // P, P])
        ys = sb("ys", [1, B])
        ext = sb("ext", [P, NK, NEXT])
        ext2 = sb("ext2", [P, NK, NEXT])
        ones = sb("ones", [P, P])
        cen = sb("cen", [P, 32])
        xsq = sb("xsq", [P, NT, P])
        xv = sb("xv", [P, 3, NT])
        wm = sb("wm", [P, 2, NK])
        w1b = sb("w1b", [P, H1])
        gg = sb("gg", [P, NK])
        xn = sb("xn", [P, NT, P])
        wk = sb("wk", [P, PR])

        p_tr = ctx.enter_context(nc.psum_tensor("p_tr", [P, 4, P], F32))
        p_ya = [ctx.enter_context(nc.psum_tensor(f"p_ya{i}", [P, 4, P], F32)) for i in range(2)]
        p_yb = [ctx.enter_context(nc.psum_tensor(f"p_yb{i}", [P, QB, PR], F32)) for i in range(2)]
        p_z = ctx.enter_context(nc.psum_tensor("p_z", [P, BLK // 8, GC], F32))
        p_m = [ctx.enter_context(nc.psum_tensor(f"p_m{i}", [P, 4, P], F32)) for i in range(2)]
        zdram = nc.dram_tensor("zdram", [NT, P, PR * GC], F32, kind="Internal").ap()

        ids_in = sem("ids_in")
        par_in = sem("par_in")
        dense_in = sem("dense_in")
        wl_in = sem("wl_in")
        w1_in = sem("w1_in")
        w1d_in = sem("w1d_in")
        w2_in = sem("w2_in")
        idx_done = sem("idx_done")
        gathered = [sem(f"gathered{k}") for k in range(QPT)]
        zeroed = sem("zeroed")
        prep = sem("prep")
        ws_done = sem("ws_done")
        bd_done = sem("bd_done")
        bw_mm = sem("bw_mm")
        bw_done = sem("bw_done")
        ext_done = sem("ext_done")
        ext_mm = sem("ext_mm")
        wl_done = sem("wl_done")
        xs_mm = sem("xs_mm")
        xs_done = sem("xs_done")
        ext_step = sem("ext_step")
        wl_scaled = sem("wl_scaled")
        wl_mean = sem("wl_mean")
        hd_mm = sem("hd_mm")
        b1_mm = sem("b1_mm")
        b1_in = sem("b1_in")
        b1_done = sem("b1_done")
        hd_done = sem("hd_done")
        x_r = sem("x_r")
        x_mm = sem("x_mm")
        x_sq = sem("x_sq")
        x_var = sem("x_var")
        x_sd = sem("x_sd")
        x_n = sem("x_n")
        x_tr = sem("x_tr")
        x_done = sem("x_done")
        tr_done = sem("tr_done")
        trE_done = sem("trE_done")
        ya_mm = sem("ya_mm")
        sqa_done = sem("sqa_done")
        va_done = sem("va_done")
        sda_done = sem("sda_done")
        ra_done = sem("ra_done")
        ya_done = sem("ya_done")
        yb_mm = sem("yb_mm")
        yb_done = sem("yb_done")
        sqb_done = sem("sqb_done")
        vb_done = sem("vb_done")
        sdb_done = sem("sdb_done")
        rb_done = sem("rb_done")
        t_done = sem("t_done")
        gram_mm = sem("gram_mm")
        zs_done = sem("zs_done")
        z_stored = [sem(f"z_stored{i}") for i in range(2)]
        z_in = sem("z_in")
        zp_done = sem("zp_done")
        zp_rest = sem("zp_rest")
        ztr_mm = sem("ztr_mm")
        zT_done = sem("zT_done")
        zT_rest = sem("zT_rest")
        lin_mm = sem("lin_mm")
        zl_done = sem("zl_done")
        sqc_done = sem("sqc_done")
        sdc_done = sem("sdc_done")
        rc_done = sem("rc_done")
        vs_done = sem("vs_done")
        var_mm = sem("var_mm")
        hs_done = sem("hs_done")
        h1_mm = sem("h1_mm")
        h1p_done = sem("h1p_done")
        h1_done = sem("h1_done")
        h2_mm = sem("h2_mm")
        h2p_done = sem("h2p_done")
        h2_done = sem("h2_done")
        y_mm = sem("y_mm")
        y_done = sem("y_done")
        y_out = sem("y_out")

        def col(name, i=0, n=1):
            a = COLS[name][0] + i
            return par[:, a:a + n]

        ident = col("ident", 0, P)
        ws = [col("ws", P * g, P) for g in range(2)]

        def pack(g):
            w = 4 * g + 4
            return (zp[:, TRI[g]:TRI[g + 1]].rearrange("p (i j) -> p i j", j=w),
                    zr[:, 4 * g:4 * g + 4, 1:1 + w])

        def has(n):
            return real(n) and (not isinstance(n, int) or n < NQ)

        def through(eng, iteration):
            iteration(0)
            iteration(1)
            with eng.Fori(2, NT) as t:
                iteration(t)
            iteration(NT)
            iteration(NT + 1)

        def phases_at(t, k):
            at = []
            for phase in reversed(range(PHASES)):
                if (k - LAG_L - phase) % QPT == 0:
                    u = t + (k - LAG_L - phase) // QPT
                    if real(u) and (not isinstance(u, int) or u < NT):
                        at.append((u, phase))
            return at

        block = ctx.enter_context(nc.Block())

        @block.sync
        def _(sp):
            sp.dma_start(ids_sb[:, :, :], ids).then_inc(ids_in, 16)
            sp.dma_start(par[:, :], params).then_inc(par_in, 16)
            sp.dma_start(dense_sb[:, :, :], dense).then_inc(dense_in, 16)
            for j in range(KEPT // P, (KEPT + DD) // P):
                sp.dma_start(w1s[:, j, :], w1[:, j, :]).then_inc(w1d_in, 16)
            for k in range(5):
                sp.wait_ge(gathered[k], 16 * len(CHUNKS[k % QPB]))
                if k == 0:
                    for j in range(KEPT // P):
                        sp.dma_start(w1s[:, j, :], w1[:, j, :]).then_inc(w1_in, 16)
                for j in {1: [0, 1], 2: [2, 3], 3: [4]}.get(k, []):
                    sp.dma_start(wl[:, j, :], wlin[:, j, :]).then_inc(wl_in, 16)
                if k == 4:
                    sp.dma_start(w2s[:, :, :], w2).then_inc(w2_in, 16)

            def tile(t):
                for half in range(4):
                    sp.wait_ge(zs_done, 4 * t + half + 1)
                    dst = zdram[t, half * 32:(half + 1) * 32, :].rearrange(
                        "(b q) (i j) -> (q i) b j", q=4, j=GC)
                    sp.dma_start(dst, zs[:, half % 2, :, :]).then_inc(z_stored[half % 2], 16)
                    sp.wait_ge(z_stored[half % 2], 16 * (2 * t + half // 2 + 1))
                    if half == 0 and (not isinstance(t, int) or t):
                        sp.wait_ge(zp_done, t)
                        sp.wait_ge(zp_rest, t)
                    sp.dma_start(zr[half * 32:(half + 1) * 32, :, :],
                                 zdram[t, half * 32:(half + 1) * 32, :].rearrange("b (i j) -> b i j", j=GC),
                                 ).then_inc(z_in, 16)

            tile(0)
            with sp.Fori(1, NT) as t:
                tile(t)
            sp.wait_ge(y_done, NT)
            sp.dma_start(out.rearrange("b o -> o b"), ys[:, :]).then_inc(y_out, 16)
            sp.wait_ge(y_out, 16)

        @block.gpsimd
        def _(pool):
            pool.wait_ge(idx_done, 1)
            for t in range(NT):
                for k in range(QPT):
                    if t:
                        pool.wait_ge(tr_done, QPT * (t - 1) + k + 1)
                    for c in CHUNKS[k % QPB]:
                        j = CPB * (k // QPB) + c
                        pool.indirect_dma_start(
                            rows[:, j, :], None, table,
                            bass.IndirectOffsetOnAxis(ap=idx[:, CPT * t + j:CPT * t + j + 1], axis=0),
                        ).then_inc(gathered[k], 16)

        @block.tensor
        def _(pe):
            def transposes(t, k):
                n = QPT * t + k
                pe.wait_ge(gathered[k], (t + 1) * (16 * len(CHUNKS[k % QPB])))
                if real(n - 1):
                    pe.wait_ge(trE_done, n)
                ch = [CPB * (k // QPB) + c for c in CHUNKS[k % QPB]]
                for u in range(2):
                    two = len(ch) > 2 * u + 1
                    src = rows[:, ch[2 * u]:ch[2 * u] + (2 if two else 1), :].rearrange("p c d -> p (c d)")
                    last = pe.transpose(p_tr[0:D * (2 if two else 1), u, :], src, ident)
                last.then_inc(tr_done, 1)

            def project_rows(t, k, n):
                if isinstance(n, int) and n == 0:
                    pe.wait_ge(ws_done, 1)
                pe.wait_ge(trE_done, n + 1)
                if real(n - 2):
                    pe.wait_ge(ya_done, n - 1)
                for i, c in enumerate(CHUNKS[k % QPB]):
                    last = pe.matmul(p_ya[k % 2][:, i, :], rowsT[:, k % 2, i // 2, :], ws[i % 2],
                                     start=True, stop=True)
                last.then_inc(ya_mm, 1)

            def project_fields(t, k, n):
                if isinstance(n, int) and n == 0:
                    pe.wait_ge(bd_done, 1)
                pe.wait_ge(ya_done, n + 1)
                if real(n - 2):
                    pe.wait_ge(yb_done, n - 1)
                q = k % QPB
                lo, hi = QB * q, QB * (q + 1)
                parts = [c for c in range(CPB) if SPAN[c][0] < hi and SPAN[c][1] > lo and c <= LAST[q]]
                for c in parts:
                    a, b = max(SPAN[c][0], lo), min(SPAN[c][1], hi)
                    own = c in CHUNKS[q]
                    kk = k if own else k - 1
                    i = CHUNKS[q].index(c) if own else CHUNKS[q - 1].index(c)
                    r = (BDCOL[c] + a - SPAN[c][0]) * PR
                    last = pe.matmul(p_yb[k % 2][:, a - lo:b - lo, :], ya[:, kk % 4, i, :],
                                     bd[:, r:r + (b - a) * PR], start=(c == parts[0]),
                                     stop=(c == parts[-1]), skip_group_check=True)
                last.then_inc(yb_mm, 1)

            def gram(t, k, n):
                pe.wait_ge(t_done, n + 1)
                if k % 2 == 0 and real(n - 2):
                    pe.wait_ge(zs_done, (4 * t + k // 2))
                q = k % QPB
                for b in range(QB * q, QB * (q + 1)):
                    last = pe.matmul(p_z[PR * (b % 4):PR * (b % 4 + 1), b % 32 // 4, :],
                                     tt[:, k // QPB % 2, b, 2:PR + 2], tt[:, k // QPB % 2, b, 0:GC],
                                     start=True, stop=True)
                last.then_inc(gram_mm, 1)

            def first_layer(u, half):
                for j in range(KEPT // P):
                    if half == 0 and j % 2 == 0:
                        pe.wait_ge(zl_done, 2 * u + j // 2 + 1)
                    for i in range(2):
                        m = 2 * half + i
                        last = pe.matmul(p_m[half][:, i, :], w1s[:, j, P * m:P * (m + 1)], zl[:, j, :],
                                         start=(i + j == 0), stop=(j == KEPT // P - 1),
                                         skip_group_check=True)
                last.then_inc(h1_mm, 1)

            def back(u, k):
                if k == 1:
                    pe.wait_ge(zp_done, u + 1)
                    pe.wait_ge(zp_rest, u + 1)
                    if real(u - 1):
                        pe.wait_ge(y_done, u)
                    for j in range(NK):
                        last = pe.transpose(p_m[j // 3][:, j % 3, :], zp[:, P * j:P * (j + 1)], ident)
                        if j in (2, NK - 1):
                            last.then_inc(ztr_mm, 1)
                if k in (2, 3, 4):
                    if k == 2:
                        pe.wait_ge(zT_done, u + 1)
                        if isinstance(u, int) and u == 0:
                            pe.wait_ge(wl_done, NK)
                    for x in range(7 * (k - 2), min(7 * (k - 1), 4 * NK)):
                        m, j = x // NK, x % NK
                        if x == 3:
                            pe.wait_ge(zT_rest, u + 1)
                        last = pe.matmul(p_m[m // 2][:, m % 2, :], wl[:, j, P * m:P * (m + 1)], zT[:, j, :],
                                         start=(j == 0), stop=(j == NK - 1))
                        if j == NK - 1 and m % 2:
                            last.then_inc(lin_mm, 1)
                if k == 5:
                    pe.wait_ge(sqc_done, 2 * u + 1)
                    first_layer(u, 0)
                    pe.wait_ge(vs_done, 3 * u + 3)
                    pe.matmul(p_m[0][:, 2, :], ones[:, :], vs[:, :], start=True, stop=True).then_inc(var_mm, 1)
                if k == 6:
                    first_layer(u, 1)
                if k == 7:
                    for m in range(H2 // P):
                        for j in range(H1 // P):
                            if m == 0 and j % 2 == 0:
                                pe.wait_ge(h1_done, 2 * u + j // 2 + 1)
                            last = pe.matmul(p_m[m][:, 0, :], w2s[:, j, P * m:P * (m + 1)], h1[:, j, :],
                                             start=(j == 0), stop=(j == H1 // P - 1))
                        last.then_inc(h2_mm, 1)
                if k == 8:
                    for j in range(H2 // P):
                        pe.wait_ge(h2_done, 2 * u + j + 1)
                        last = pe.matmul(p_m[0][0:1, 1, :], col("w3", j), h2[:, j, :],
                                         start=(j == 0), stop=(j == H2 // P - 1))
                    last.then_inc(y_mm, 1)

            def first_steps(n):
                if n == 1:
                    pe.wait_ge(prep, 2)
                    for t in range(NT):
                        for j in range(2):
                            last = pe.matmul(p_m[0][:, t, :], dense_sb[:, j, P + P * t:P + P * (t + 1)],
                                             dense_sb[:, j, 0:P], start=(j == 0), stop=(j == 1))
                    last.then_inc(x_mm, 1)
                    pe.matmul(p_m[1][:, 0, 0:PR], col("bs", 0, P), wk[:, :], start=True,
                              stop=True).then_inc(bw_mm, 1)
                if n == 2:
                    pe.wait_ge(bw_done, 1)
                    pe.wait_ge(x_n, 1)
                    for t in range(NT):
                        last = pe.transpose(p_m[1][:, t, :], xn[:, t, :], ident)
                    last.then_inc(x_tr, 1)
                if n == 3:
                    pe.wait_ge(x_done, 1)
                    for t in range(NT):
                        last = pe.matmul(p_m[1][:, 0, t:t + 1], xT[:, P * t:P * (t + 1)], ones[:, 0:1],
                                         start=True, stop=True)
                    last.then_inc(xs_mm, 1)
                if n == 4:
                    pe.wait_ge(b1_in, KEPT // P)
                    pe.wait_ge(xs_done, 1)
                    for m in range(H1 // P):
                        last = pe.matmul(p_m[1][:, m, 0:1], w1b[:, P * m:P * (m + 1)], ones[:, 0:1],
                                         start=True, stop=True)
                    last.then_inc(b1_mm, 1)
                for m, (bank, steps) in enumerate(HD):
                    if n not in steps:
                        continue
                    j = steps.index(n)
                    if (m, j) == (0, 0):
                        pe.wait_ge(w1d_in, 32)
                        pe.wait_ge(x_n, 1)
                    if (m, j) == (1, 0):
                        pe.wait_ge(b1_done, 1)
                    if (m, j) == (2, 0):
                        pe.wait_ge(hd_done, 2)
                    if (m, j) == (3, 0):
                        pe.wait_ge(wl_scaled, 1)
                    mm = pe.matmul(p_m[bank][:, :, :], w1s[:, KEPT // P + j, P * m:P * (m + 1)],
                                   dense_sb[:, j, P:P + B], start=(j == 0), stop=(j == 1))
                    if j == 1:
                        mm.then_inc(hd_mm, 1)
                if n == LIN:
                    pe.wait_ge(ext_done, 1)
                    pe.wait_ge(wl_in, 16 * NK)
                    pe.wait_ge(hd_done, 1)
                    for j in range(NK):
                        last = pe.matmul(p_m[0][EXT:EXT + NEXT, :, :], ext[:, j, :], wl[:, j, :],
                                         start=(j == 0), stop=(j == NK - 1))
                    last.then_inc(ext_mm, 1)
                if n == 12:
                    pe.wait_ge(w1_in, 16 * (KEPT // P))
                    pe.wait_ge(w2_in, 16)

            def iteration(t):
                for k in range(QPT):
                    n = QPT * t + k
                    if has(n - LAG_G):
                        gram(t, k - LAG_G, n - LAG_G)
                    if has(n - LAG_A):
                        project_rows(t, k - LAG_A, n - LAG_A)
                    if has(n):
                        transposes(t, k)
                    if has(n - LAG_B):
                        project_fields(t, k - LAG_B, n - LAG_B)
                    if isinstance(t, int) and n < 2 * QPT:
                        first_steps(n)
                    for u, phase in phases_at(t, k):
                        back(u, phase)

            pe.wait_ge(zeroed, 5)
            pe.wait_ge(par_in, 16)
            for _ in range(3):
                pe.matmul(p_tr[:, :, :], ident, par[:, 0:4 * P], start=True, stop=True)
            through(pe, iteration)

        @block.scalar
        def _(act):
            def evacuate_rows(t, k, n):
                act.wait_ge(tr_done, n + 1)
                if real(n - 2):
                    act.wait_ge(ya_mm, n - 1)
                if len(CHUNKS[k % QPB]) == 4:
                    act.activation(rowsT[:, k % 2, :, :], p_tr[:, 0:2, :], ACT.Copy).then_inc(trE_done, 1)
                else:
                    act.activation(rowsT[:, k % 2, 0, :], p_tr[:, 0, :], ACT.Copy)
                    act.activation(rowsT[0:D, k % 2, 1, :], p_tr[0:D, 1, :], ACT.Copy).then_inc(trE_done, 1)

            def square_rows(t, k, n):
                m = len(CHUNKS[k % QPB])
                act.wait_ge(ya_mm, n + 1)
                if real(n - 2):
                    act.wait_ge(va_done, n - 1)
                act.activation(sqa[:, k % 2, 0:m, :], p_ya[k % 2][:, 0:m, :], ACT.Square).then_inc(sqa_done, 1)

            def square_fields(t, k, n):
                act.wait_ge(yb_done, n + 1)
                if real(n - 2):
                    act.wait_ge(vb_done, n - 1)
                act.activation(sqb[:, k % 2, :, :], yb[:, k % 4, :, :], ACT.Square).then_inc(sqb_done, 1)

            def deviation_rows(t, k, n):
                m = len(CHUNKS[k % QPB])
                act.wait_ge(va_done, n + 1)
                act.activation(sda[:, k % 2, 0:m], va[:, k % 2, 0:m], ACT.Sqrt, bias=eps[:, 0:1],
                               scale=1.0 / E).then_inc(sda_done, 1)

            def normalise_rows(t, k, n):
                m = len(CHUNKS[k % QPB])
                act.wait_ge(ra_done, n + 1)
                if real(n - 4):
                    act.wait_ge(yb_mm, n - 2)
                for i in range(m):
                    last = act.activation(ya[:, k % 4, i, :], p_ya[k % 2][:, i, :], ACT.Copy,
                                          scale=ra[:, k % 2, i:i + 1])
                last.then_inc(ya_done, 1)

            def deviation_fields(t, k, n):
                act.wait_ge(vb_done, n + 1)
                if real(n - 2):
                    act.wait_ge(rb_done, n - 1)
                act.activation(sdb[:, k % 2, :], vb[:, k % 2, :], ACT.Sqrt, bias=eps[:, 0:1],
                               scale=1.0 / PR).then_inc(sdb_done, 1)

            def evacuate_gram(t, k, n):
                half = k // 2
                act.wait_ge(gram_mm, n + 1)
                if real(n - 4):
                    act.wait_ge(z_stored[half % 2], 16 * (2 * t + half // 2))
                act.activation(zs[:, half % 2, :, :], p_z[:, :, :], ACT.Copy).then_inc(zs_done, 1)

            def back(u, k):
                if k == 0:
                    act.wait_ge(z_in, 64 * (u + 1))
                    if real(u - 1):
                        act.wait_ge(ztr_mm, 2 * u)
                    for g in (PR // 4 - 2, PR // 4 - 1):
                        act.activation(*pack(g), ACT.Copy)
                    act.activation(zp[:, HS:HS + PR], zr[:, :, 0], ACT.Copy).then_inc(zp_rest, 1)
                if k == 1:
                    act.wait_ge(ztr_mm, 2 * u + 1)
                    act.activation(zT[:, 0:3, :], p_m[0][:, 0:3, :], ACT.Copy).then_inc(zT_done, 1)
                if k in (3, 4):
                    half = k - 3
                    act.wait_ge(lin_mm, 2 * u + half + 1)
                    chunks = [j for j in (2 * half, 2 * half + 1) if j < KEPT // P]
                    if half == 1:
                        act.activation(sqc[:, 2:4, :], p_m[1][:, 0:2, :], ACT.Square).then_inc(sqc_done, 1)
                    for j in chunks:
                        last = act.activation(zl[:, j, :], p_m[half][:, j % 2, :], ACT.Copy, scale=col("gl", j))
                    last.then_inc(zl_done, 1)
                    if half == 0:
                        act.activation(sqc[:, 0:2, :], p_m[0][:, 0:2, :], ACT.Square).then_inc(sqc_done, 1)
                if k == 6:
                    act.wait_ge(var_mm, u + 1)
                    act.activation(sdc[:, :], p_m[0][:, 2, :], ACT.Sqrt, bias=eps[:, 0:1],
                                   scale=1.0 / MAXD).then_inc(sdc_done, 1)
                    for half in range(2):
                        act.wait_ge(h1p_done, 2 * u + half + 1)
                        act.activation(h1[:, 2 * half:2 * half + 2, :], h1p[:, 2 * half:2 * half + 2, :],
                                       ACT.Relu).then_inc(h1_done, 1)
                if k == 7:
                    for m in range(H2 // P):
                        act.wait_ge(h2p_done, 2 * u + m + 1)
                        act.activation(h2[:, m, :], h2p[:, m, :], ACT.Relu).then_inc(h2_done, 1)

            def first_steps(n):
                if n == 1:
                    act.wait_ge(x_mm, 1)
                    act.activation(xsq[:, :, :], p_m[0][:, :, :], ACT.Square).then_inc(x_sq, 1)
                    act.wait_ge(x_var, 1)
                    act.activation(xv[:, 1, :], xv[:, 0, :], ACT.Sqrt, bias=eps[:, 0:1],
                                   scale=1.0 / E).then_inc(x_sd, 1)
                if LIN < n <= LIN + NK:
                    j = LIN_CHUNKS[n - LIN - 1]
                    act.wait_ge(ext_mm, 1)
                    full = P if j < NK - 1 else EXT
                    act.wait_ge(ext_done, 1)
                    if j == NK - 1:
                        act.activation(wl[EXT:EXT + NEXT, j, :], p_m[0][EXT:EXT + NEXT, :, :], ACT.Copy,
                                       scale=col("ext")[EXT:EXT + NEXT],
                                       accum_out=wm[EXT:EXT + NEXT, 0, j:j + 1])
                    act.activation(wl[0:full, j, :], wl[0:full, j, :], ACT.Copy, scale=gg[0:full, j:j + 1],
                                   accum_out=wm[0:full, 0, j:j + 1]).then_inc(wl_scaled, 1)
                for m, (bank, steps) in enumerate(HD):
                    if n == steps[1]:
                        act.wait_ge(hd_mm, m + 1)
                        if m == 0:
                            act.wait_ge(b1_done, 1)
                        act.activation(hd[:, m, :], p_m[bank][:, :, :], ACT.Identity,
                                       bias=b1[:, m:m + 1]).then_inc(hd_done, 1)

            def iteration(t):
                for k in range(QPT):
                    n = QPT * t + k
                    if has(n - LAG_AN):
                        deviation_rows(t, k - LAG_AN, n - LAG_AN)
                    if has(n - LAG_G) and (k - LAG_G) % 2:
                        evacuate_gram(t, k - LAG_G, n - LAG_G)
                    if has(n - LAG_A):
                        square_rows(t, k - LAG_A, n - LAG_A)
                    if has(n):
                        evacuate_rows(t, k, n)
                    if has(n - LAG_AN):
                        normalise_rows(t, k - LAG_AN, n - LAG_AN)
                    if has(n - LAG_BS):
                        deviation_fields(t, k - LAG_BS, n - LAG_BS)
                    for u, phase in phases_at(t, k):
                        back(u, phase)
                    if isinstance(t, int) and n < 2 * QPT:
                        first_steps(n)
                    if has(n - LAG_B):
                        square_fields(t, k - LAG_B, n - LAG_B)

            act.wait_ge(zeroed, 2)
            act.activation(sdc[:, 0:1], eps[:, :], ACT.Sqrt)
            act.wait_ge(par_in, 16)
            through(act, iteration)

        @block.vector
        def _(dve):
            def sum_rows(t, k, n):
                m = len(CHUNKS[k % QPB])
                dve.wait_ge(sqa_done, n + 1)
                dve.tensor_reduce(va[:, k % 2, 0:m], sqa[:, k % 2, 0:m, :], AX.X, ALU.add).then_inc(va_done, 1)

            def scale_rows(t, k, n):
                m = len(CHUNKS[k % QPB])
                dve.wait_ge(sda_done, n + 1)
                if real(n - 2):
                    dve.wait_ge(ya_done, n - 1)
                dve.reciprocal(ra[:, k % 2, 0:m], sda[:, k % 2, 0:m]).then_inc(ra_done, 1)

            def affine_fields(t, k, n):
                dve.wait_ge(yb_mm, n + 1)
                if real(n - 4):
                    dve.wait_ge(t_done, n - 3)
                dve.scalar_tensor_tensor(
                    out=yb[:, k % 4, :, :], in0=p_yb[k % 2][:, :, :], scalar=col("gs"),
                    in1=bw[:, None, :].to_broadcast([P, QB, PR]), op0=ALU.mult, op1=ALU.add,
                ).then_inc(yb_done, 1)

            def sum_fields(t, k, n):
                dve.wait_ge(sqb_done, n + 1)
                dve.tensor_reduce(vb[:, k % 2, :], sqb[:, k % 2, :, :], AX.X, ALU.add).then_inc(vb_done, 1)

            def normalise_fields(t, k, n):
                dve.wait_ge(sdb_done, n + 1)
                dve.reciprocal(rb[:, k % 2, :], sdb[:, k % 2, :]).then_inc(rb_done, 1)
                dve.wait_ge(rb_done, n + 1)
                half, q = (k // QPB) % 2, k % QPB
                if q == 0:
                    blk = 2 * t + k // QPB
                    if real(n - 2 * QPB):
                        dve.wait_ge(gram_mm, n - QPB)
                    dve.tensor_copy(tt[:, half, :, 1], xT[:, bass.ds(BLK * blk, BLK)])
                dve.tensor_tensor(tt[:, half, QB * q:QB * (q + 1), 2:PR + 2], yb[:, k % 4, :, :],
                                  rb[:, k % 2, :, None].to_broadcast([P, QB, PR]), ALU.mult).then_inc(t_done, 1)

            def back(u, k):
                if k == 0:
                    dve.wait_ge(z_in, 64 * (u + 1))
                    if real(u - 1):
                        dve.wait_ge(ztr_mm, 2 * u)
                    for g in range(PR // 4 - 2):
                        dve.tensor_copy(*pack(g))
                    dve.tensor_copy(zp[:, HS + PR:HS + PR + 1], xs[:, bass.ds(u, 1)]).then_inc(zp_done, 1)
                if k == 1:
                    dve.wait_ge(ztr_mm, 2 * u + 2)
                    dve.tensor_copy(zT[:, 3:5, :], p_m[1][:, 0:2, :]).then_inc(zT_rest, 1)
                if k == 3:
                    dve.wait_ge(sqc_done, 2 * u + 1)
                    dve.tensor_tensor(vs[:, :], sqc[:, 0, :], sqc[:, 1, :], ALU.add).then_inc(vs_done, 1)
                if k == 4:
                    dve.wait_ge(sqc_done, 2 * u + 2)
                    for j in (2, 3):
                        dve.wait_ge(vs_done, 3 * u + j - 1)
                        dve.tensor_tensor(vs[:, :], vs[:, :], sqc[:, j, :], ALU.add).then_inc(vs_done, 1)
                if k == 6:
                    dve.wait_ge(sdc_done, u + 1)
                    halves = [slice(0, 2), slice(2, 4)]
                    for m in halves:
                        dve.tensor_tensor(hs[:, m, :], hd[:, m, bass.ds(P * u, P)],
                                          sdc[:, None, :].to_broadcast([P, 2, P]), ALU.mult).then_inc(hs_done, 1)
                    for half, m in enumerate(halves):
                        dve.wait_ge(hs_done, 2 * u + half + 1)
                        dve.wait_ge(h1_mm, 2 * u + half + 1)
                        dve.tensor_tensor(h1p[:, m, :], p_m[half][:, 0:2, :], hs[:, m, :],
                                          ALU.add).then_inc(h1p_done, 1)
                if k == 7:
                    dve.reciprocal(rc[:, :], sdc[0:1, :]).then_inc(rc_done, 1)
                    for m in range(H2 // P):
                        dve.wait_ge(h2_mm, 2 * u + m + 1)
                        dve.scalar_tensor_tensor(out=h2p[:, m, :], in0=sdc[:, :], scalar=col("b2", m),
                                                 in1=p_m[m][:, 0, :], op0=ALU.mult,
                                                 op1=ALU.add).then_inc(h2p_done, 1)
                if k == 8:
                    dve.wait_ge(y_mm, u + 1)
                    dve.wait_ge(rc_done, u + 1)
                    dve.tensor_tensor(ys[:, bass.ds(P * u, P)], p_m[0][0:1, 1, :], rc[:, :],
                                      ALU.mult).then_inc(y_done, 1)

            def first_steps(n):
                if n == 1:
                    dve.wait_ge(bw_mm, 1)
                    dve.tensor_copy(bw[:, :], p_m[1][:, 0, 0:PR]).then_inc(bw_done, 1)
                    dve.wait_ge(bw_done, 1)
                    dve.wait_ge(x_sq, 1)
                    dve.tensor_reduce(xv[:, 0, :], xsq[:, :, :], AX.X, ALU.add).then_inc(x_var, 1)
                    dve.wait_ge(x_sd, 1)
                    dve.reciprocal(xv[:, 2, :], xv[:, 1, :]).then_inc(x_r, 1)
                    dve.wait_ge(x_r, 1)
                    dve.tensor_tensor(xn[:, :, :], p_m[0][:, :, :], xv[:, 2, :, None].to_broadcast([P, NT, P]),
                                      ALU.mult).then_inc(x_n, 1)
                if n == 2:
                    dve.wait_ge(x_tr, 1)
                    dve.tensor_scalar(xT[:, :], p_m[1][:, :, :], col("gd"), col("bd"), ALU.mult,
                                      ALU.add).then_inc(x_done, 1)
                if n == 3:
                    dve.wait_ge(x_done, 1)
                    dve.wait_ge(xs_mm, 1)
                    dve.tensor_copy(xs[:, :], p_m[1][:, 0, 0:NT]).then_inc(xs_done, 1)
                    dve.wait_ge(xs_done, 1)
                    dve.wait_ge(w1_in, 16 * (KEPT // P))
                    dve.tensor_scalar(w1b[:, :], w1s[:, 0, :], col("bl", 0), None, ALU.mult).then_inc(b1_in, 1)
                    for j in range(1, KEPT // P):
                        dve.wait_ge(b1_in, j)
                        dve.scalar_tensor_tensor(out=w1b[:, :], in0=w1s[:, j, :], scalar=col("bl", j),
                                                 in1=w1b[:, :], op0=ALU.mult, op1=ALU.add).then_inc(b1_in, 1)
                if n == 4:
                    dve.wait_ge(b1_mm, 1)
                    dve.tensor_tensor(b1[:, :], p_m[1][:, :, 0], col("b1", 0, H1 // P), ALU.add).then_inc(b1_done, 1)
                    pair = [col("pair", NK * i, NK) for i in range(4)]
                    mi = col("mi", 0, NK * NEXT).rearrange("p (c r) -> p c r", r=NEXT)
                    mj = col("mj", 0, NK * NEXT).rearrange("p (c r) -> p c r", r=NEXT)
                    dve.tensor_tensor(gg[:, :], pair[2], pair[3], ALU.mult).then_inc(ext_step, 1)
                    dve.tensor_tensor(ext[:, :, :], mi, pair[1][:, :, None].to_broadcast([P, NK, NEXT]),
                                      ALU.mult).then_inc(ext_step, 1)
                    dve.tensor_tensor(ext2[:, :, :], mj, pair[0][:, :, None].to_broadcast([P, NK, NEXT]),
                                      ALU.mult).then_inc(ext_step, 1)
                    dve.wait_ge(ext_step, 3)
                    dve.tensor_tensor(ext[:, :, NEXT - 1], ext[:, :, NEXT - 1], pair[0],
                                      ALU.mult).then_inc(ext_step, 1)
                    dve.wait_ge(ext_step, 4)
                    dve.tensor_tensor(ext[:, :, :], ext[:, :, :], ext2[:, :, :], ALU.add).then_inc(ext_done, 1)
                if LIN < n <= LIN + NK:
                    j = LIN_CHUNKS[n - LIN - 1]
                    dve.wait_ge(wl_scaled, n - LIN)
                    dve.tensor_scalar(wm[:, 1, j:j + 1], wm[:, 0, j:j + 1], 1.0 / MAXD, None,
                                      ALU.mult).then_inc(wl_mean, 1)
                    dve.wait_ge(wl_mean, n - LIN)
                    dve.tensor_scalar(wl[:, j, :], wl[:, j, :], wm[:, 1, j:j + 1], None,
                                      ALU.subtract).then_inc(wl_done, 1)

            def iteration(t):
                for k in range(QPT):
                    n = QPT * t + k
                    if has(n - LAG_AN):
                        scale_rows(t, k - LAG_AN, n - LAG_AN)
                    if has(n - LAG_BS):
                        sum_fields(t, k - LAG_BS, n - LAG_BS)
                    if has(n - LAG_A):
                        sum_rows(t, k - LAG_A, n - LAG_A)
                    if has(n - LAG_B):
                        affine_fields(t, k - LAG_B, n - LAG_B)
                    for u, phase in phases_at(t, k):
                        back(u, phase)
                    if has(n - LAG_BN):
                        normalise_fields(t, k - LAG_BN, n - LAG_BN)
                    if isinstance(t, int) and n < 2 * QPT:
                        first_steps(n)

            def centre(view, n, over):
                steps[0] += 2
                dve.tensor_reduce(cen[:, 0:n], view, AX.X, ALU.add).then_inc(prep_in, 1)
                dve.wait_ge(prep_in, steps[0] - 1)
                dve.tensor_scalar(cen[:, 0:n], cen[:, 0:n], 1.0 / over, None, ALU.mult).then_inc(prep_in, 1)
                dve.wait_ge(prep_in, steps[0])
                return dve.tensor_tensor(view, view, cen[:, 0:n, None].to_broadcast([P, n, over]), ALU.subtract)

            prep_in = sem("prep_in")
            steps = [0]
            dve.memset(rowsT[:, :, :, :], 0.0).then_inc(zeroed, 1)
            dve.memset(eps[:, :], EPS).then_inc(zeroed, 1)
            dve.memset(ones[:, :], 1.0).then_inc(zeroed, 1)
            dve.memset(tt[:, :, :, 0], 1.0).then_inc(zeroed, 1)
            dve.memset(zp[:, HS + PR:HS + PR + 2], 1.0)
            dve.memset(wm[:, :, :], 0.0)
            dve.memset(zp[:, HS + NEXT:], 0.0).then_inc(zeroed, 1)
            dve.wait_ge(ids_in, 16)
            dve.tensor_tensor(idx[:, :], ids_sb[:, 0, :], ids_sb[:, 1, :], ALU.add).then_inc(idx_done, 1)

            dve.wait_ge(par_in, 16)
            centre(col("ws", 0, 2 * P).rearrange("p (g e) -> p g e", g=2), 2, P).then_inc(ws_done, 1)
            dve.wait_ge(ws_done, 1)
            wsi = col("wsi", 0, CPB * PR).rearrange("p (c r) -> p c r", r=PR)
            centre(wsi, CPB, PR).then_inc(prep_in, 1)
            steps[0] += 1
            dve.wait_ge(prep_in, steps[0])
            dve.tensor_scalar(wk[:, :], wsi[:, 0, :], col("mask"), None, ALU.mult).then_inc(prep, 1)
            for c in range(CPB):
                m = BDCOL[c + 1] - BDCOL[c]
                v = bd[:, BDCOL[c] * PR:BDCOL[c + 1] * PR].rearrange("p (b r) -> p b r", r=PR)
                last = dve.tensor_tensor(v, wsi[:, c, None, :].to_broadcast([P, m, PR]),
                                         col("mask", BDCOL[c], m)[:, :, None].to_broadcast([P, m, PR]), ALU.mult)
            last.then_inc(bd_done, 1)
            dve.wait_ge(dense_in, 16)
            centre(dense_sb[:, :, 0:P], 2, P).then_inc(prep, 1)
            through(dve, iteration)


def layout(x):
    f = np.float32
    row = np.arange(CPB * P)
    field = (row % NF).reshape(CPB, P)
    off = np.cumsum([0] + VOCAB)[:NF].astype(np.int32)
    offs = np.tile(off, B).reshape(NT * CPT, P).T
    ids = np.asarray(x["ids"]).reshape(NT * CPT, P).T
    table = np.concatenate([np.asarray(x[f"tbl_{i}"]) for i in range(NF)], axis=0)
    mask = np.zeros((P, NCOL), f)
    for c, (a, b) in enumerate(SPAN):
        sample = (P * c + np.arange(P)) // NF
        for s in range(a, b):
            mask[:, BDCOL[c] + s - a] = sample == s
    wsT = np.zeros((P, 2, P), f)
    wst = np.asarray(x["L0_rec_Ws"]).T
    wsT[:D, 0], wsT[D:, 1] = wst, wst
    wsiT = np.asarray(x["L0_rec_Wsi"]).T
    g, o = np.asarray(x["L0_rec_gsi"]), np.asarray(x["L0_rec_bsi"])
    pair = np.zeros((P, 4, NK), f)
    mi, mj = np.zeros((NK, P, NEXT), f), np.zeros((NK, P, NEXT), f)
    for s, ij in enumerate(pairs()):
        if ij is None:
            continue
        c, r, (i, j) = s // P, s % P, ij
        pair[r, 0, c], pair[r, 2, c], pair[r, 3, c] = o[i], g[i], 1
        mj[c, r, j - 1 if j else PR] = 1
        if j:
            pair[r, 1, c], pair[r, 3, c] = o[j - 1], g[j - 1]
            mi[c, r, i], mi[c, r, NEXT - 1] = 1, E
    ext = np.zeros((P, 1), f)
    ext[EXT:EXT + NEXT, 0] = 1
    ext[EXT:EXT + PR, 0] = g
    columns = {
        "gs": np.asarray(x["L0_rec_gs"])[:, None], "gd": np.asarray(x["L0_rec_gd"])[:, None],
        "bd": np.asarray(x["L0_rec_bd"])[:, None],
        "gl": np.asarray(x["L0_rec_gl"])[:KEPT].reshape(-1, P).T,
        "bl": np.asarray(x["L0_rec_bl"])[:KEPT].reshape(-1, P).T,
        "b1": np.asarray(x["b_top1"]).reshape(-1, P).T, "b2": np.asarray(x["b_top2"]).reshape(-1, P).T,
        "w3": np.asarray(x["W_top3"])[:, 0].reshape(-1, P).T,
        "pair": pair.reshape(P, 4 * NK), "ext": ext,
        "mi": mi.transpose(1, 0, 2).reshape(P, -1), "mj": mj.transpose(1, 0, 2).reshape(P, -1),
        "bs": np.broadcast_to(np.asarray(x["L0_rec_bs"]), (P, P)),
        "ident": np.eye(P, dtype=f), "mask": mask,
        "wsi": wsiT[field].transpose(1, 0, 2).reshape(P, CPB * PR), "ws": wsT.reshape(P, 2 * P),
    }
    params = np.concatenate([columns[k] for k in COLS], axis=1)
    wd = np.asarray(x["L0_rec_Wd"]).T.reshape(2, P, P)
    de = np.asarray(x["r_dense_t"]).T.reshape(2, P, B)
    dense = np.concatenate([wd, de], axis=2).transpose(1, 0, 2)
    wlT = np.asarray(x["L0_rec_Wl"]).T
    wlin = np.zeros((NK * P, MAXD), f)
    for r, ij in enumerate(pairs()):
        if ij is not None:
            wlin[r] = wlT[ij[0] * (ij[0] + 1) // 2 + ij[1]]
    w1 = np.asarray(x["W_top1"])
    w1 = np.concatenate([w1[:KEPT], w1[MAXD:]], axis=0)
    return {
        "ids": np.stack([ids, offs], axis=1), "table": table, "params": params, "dense": dense,
        "wlin": wlin.reshape(NK, P, MAXD).transpose(1, 0, 2),
        "w1": w1.reshape(-1, P, H1).transpose(1, 0, 2),
        "w2": np.asarray(x["W_top2"]).reshape(-1, P, H2).transpose(1, 0, 2),
    }


def kernel(**inputs):
    import concourse.bacc as bacc
    from concourse.bass_utils import run_bass_kernel_spmd

    nc = bacc.Bacc("TRN2", target_bir_lowering=False, num_devices=1)
    arrays, args = {}, []
    for name, a in layout(inputs).items():
        a = np.ascontiguousarray(a)
        arrays[f"in_{name}"] = a
        args.append(nc.dram_tensor(f"in_{name}", a.shape, mybir.dt.from_np(a.dtype), kind="ExternalInput").ap())
    args.append(nc.dram_tensor("out_y", (B, 1), F32, kind="ExternalOutput").ap())
    dlrm(nc, *args)
    r = run_bass_kernel_spmd(nc, [arrays], core_ids=[0])
    return r.results[0]["out_y"]
```
